# Optimizing a Trainium2 kernel written in Bass

```python
import numpy as np
import jax
import jax.numpy as jnp

def _softmax(x, axis=-1):
    return jax.nn.softmax(x, axis=axis)

def _gelu(x):
    return jax.nn.gelu(x, approximate=True)

def _silu(x):
    return jax.nn.silu(x)

def _sigmoid(x):
    return jax.nn.sigmoid(x)

def _layernorm(x, axis=-1, eps=1e-05):
    m = jnp.mean(x, axis=axis, keepdims=True)
    v = jnp.var(x, axis=axis, keepdims=True)
    return (x - m) / jnp.sqrt(v + eps)

def _scatter_add(tgt, idx, src, axis=0):
    return tgt.at[idx].add(src)

def _segment_sum(src, seg, n):
    return jax.ops.segment_sum(src, seg, n)
kernel_name = 'mk_flamingo_gated_d1_seqx_r4_9703c6'

def setup_inputs(seed: int=0):
    np.random.seed(seed)
    _w = jnp.asarray

    def _rec_inputs():
        import jax
        import jax.numpy as jnp
        _rk = jax.random.key(seed)
        x = 0.0003765 + 1 * jax.random.normal(jax.random.fold_in(_rk, 1), (8, 256, 512), jnp.float32)
        _lenS = 256 - jax.random.randint(jax.random.fold_in(_rk, 7), (8,), 0, max(1, 256 // 4) + 1, jnp.int32)
        _lenS2 = 256 - jax.random.randint(jax.random.fold_in(_rk, 8), (8,), 0, max(1, 256 // 4) + 1, jnp.int32)
        _ctx_2048P = jax.random.normal(jax.random.fold_in(_rk, 11), (8, 16, 512), jnp.float32)
        _ctx_2048c = jax.random.dirichlet(jax.random.fold_in(_rk, 511), 0.3 * jnp.ones((16,), jnp.float32), (8, 256))
        _ctx_2048t = jnp.einsum('bsk,bkd->bsd', _ctx_2048c, _ctx_2048P)
        _ctx_2048t = _ctx_2048t * jax.lax.rsqrt(jnp.mean(jnp.square(_ctx_2048t)) + 1e-12) * 0.953939
        ctx_2048 = -0.000292821 + 1.00034 * (_ctx_2048t + 0.3 * jax.random.normal(jax.random.fold_in(_rk, 611), (8, 256, 512), jnp.float32))
        _g = jax.random.normal(jax.random.fold_in(_rk, 9001), (2, 1), jnp.float32)
        _g = jnp.sign(_g) * jnp.maximum(jnp.abs(_g), 1.0) + (_g == 0) * 1.0
        g_xattn = _g[0]
        g_ffn = _g[1]
        return (x, ctx_2048, g_xattn, g_ffn)
    x, ctx_2048, g_xattn, g_ffn = _rec_inputs()

    def _L0_xattn_setup():
        import jax, jax.numpy as jnp
        import numpy as np
        key = jax.random.key(seed)
        k1, k2, k3, k4, k5 = jax.random.split(key, 5)
        B, D_MODEL, L = (2, 256, 512)
        HEAD_DIM = 8
        H = D_MODEL // HEAD_DIM
        return {'k': jax.random.normal(k1, (B, D_MODEL, L), dtype=jnp.float32), 'v': jax.random.normal(k2, (B, D_MODEL, L), dtype=jnp.float32), 'q': jax.random.normal(k3, (B, D_MODEL, L), dtype=jnp.float32), 'ssm_kernel': jax.random.normal(k4, (H, L), dtype=jnp.float32), 'D': jax.random.normal(k5, (H,), dtype=jnp.float32), 'head_dim': HEAD_DIM}
    _L0_xattn_all = _L0_xattn_setup()
    _L0_xattn_in = {k: v for k, v in _L0_xattn_all.items() if k in ('ssm_kernel', 'D')}
    del _L0_xattn_all

    def _L0_ffn_setup():
        import jax, jax.numpy as jnp
        import numpy as np
        N_BLOCKS = 6
        DIM = 512
        HIDDEN = 4 * DIM
        LN_EPS = 1e-05
        W_SCALE = 0.02

        def _block(x, w1, b1, w2, b2):
            h = jax.nn.gelu(jnp.einsum('bsd,hd->bsh', x, w1) + b1, approximate=False)
            return jnp.einsum('bsh,dh->bsd', h, w2) + b2 + x

        def _layernorm(x, g, b):
            mu = jnp.mean(x, axis=-1, keepdims=True)
            var = jnp.mean(jnp.square(x - mu), axis=-1, keepdims=True)
            return (x - mu) * jax.lax.rsqrt(var + LN_EPS) * g + b
        key = jax.random.key(seed)
        ks = jax.random.split(key, 4)
        x = jax.random.normal(ks[0], (4, 512, DIM), dtype=jnp.float32)
        W1 = jax.random.normal(ks[1], (N_BLOCKS, HIDDEN, DIM), dtype=jnp.float32) * W_SCALE
        B1 = jnp.zeros((N_BLOCKS, HIDDEN), dtype=jnp.float32)
        W2 = jax.random.normal(ks[2], (N_BLOCKS, DIM, HIDDEN), dtype=jnp.float32) * W_SCALE
        B2 = jnp.zeros((N_BLOCKS, DIM), dtype=jnp.float32)
        LN_G = jnp.ones((N_BLOCKS - 1, DIM), dtype=jnp.float32)
        LN_B = jnp.zeros((N_BLOCKS - 1, DIM), dtype=jnp.float32)
        return {'x': x, 'W1': W1, 'B1': B1, 'W2': W2, 'B2': B2, 'LN_G': LN_G, 'LN_B': LN_B}
    _L0_ffn_all = _L0_ffn_setup()
    _L0_ffn_in = {k: v for k, v in _L0_ffn_all.items() if k in ('W1', 'B1', 'W2', 'B2', 'LN_G', 'LN_B')}
    del _L0_ffn_all
    return {'x': x, 'ctx_2048': ctx_2048, 'g_xattn': g_xattn, 'g_ffn': g_ffn, 'L0_xattn_ssm_kernel': _L0_xattn_in['ssm_kernel'], 'L0_xattn_D': _L0_xattn_in['D'], 'L0_ffn_W1': _L0_ffn_in['W1'], 'L0_ffn_B1': _L0_ffn_in['B1'], 'L0_ffn_W2': _L0_ffn_in['W2'], 'L0_ffn_B2': _L0_ffn_in['B2'], 'L0_ffn_LN_G': _L0_ffn_in['LN_G'], 'L0_ffn_LN_B': _L0_ffn_in['LN_B']}

def reference(x, ctx_2048, g_xattn, g_ffn, L0_xattn_ssm_kernel, L0_xattn_D, L0_ffn_W1, L0_ffn_B1, L0_ffn_W2, L0_ffn_B2, L0_ffn_LN_G, L0_ffn_LN_B):
    import jax
    import jax.numpy as jnp

    def _L0_xattn_ref(k, v, q, ssm_kernel, D, head_dim):
        import jax, jax.numpy as jnp
        import numpy as np
        B, HD, L = k.shape
        H = HD // head_dim
        fft_size = 2 * L
        k_ = k.reshape(B, H, head_dim, L)
        v_ = v.reshape(B, H, head_dim, L)
        q_ = q.reshape(B, H, head_dim, L)
        kv = jnp.einsum('bhil,bhjl->bijhl', k_, v_)
        kv_f = jnp.fft.rfft(kv, n=fft_size)
        kernel_f = jnp.fft.rfft(ssm_kernel, n=fft_size)
        y = jnp.fft.irfft(kv_f * kernel_f, n=fft_size)[..., :L]
        out = y + kv * D[None, None, None, :, None]
        out = jnp.einsum('bijhl,bhil->bjhl', out, q_)
        out = jnp.transpose(out, (0, 2, 1, 3)).reshape(B, H * head_dim, L)
        return out.astype(k.dtype)

    def _L0_ffn_ref(x, W1, B1, W2, B2, LN_G, LN_B):
        import jax, jax.numpy as jnp
        import numpy as np
        N_BLOCKS = 6
        DIM = 512
        HIDDEN = 4 * DIM
        LN_EPS = 1e-05
        W_SCALE = 0.02

        def _block(x, w1, b1, w2, b2):
            h = jax.nn.gelu(jnp.einsum('bsd,hd->bsh', x, w1) + b1, approximate=False)
            return jnp.einsum('bsh,dh->bsd', h, w2) + b2 + x

        def _layernorm(x, g, b):
            mu = jnp.mean(x, axis=-1, keepdims=True)
            var = jnp.mean(jnp.square(x - mu), axis=-1, keepdims=True)
            return (x - mu) * jax.lax.rsqrt(var + LN_EPS) * g + b
        for i in range(N_BLOCKS):
            x = _block(x, W1[i], B1[i], W2[i], B2[i])
            if i < N_BLOCKS - 1:
                x = _layernorm(x, LN_G[i], LN_B[i])
        return x
    x = x + jnp.tanh(g_xattn[0]) * _L0_xattn_ref(ctx_2048, ctx_2048, _layernorm(x, axis=-1), L0_xattn_ssm_kernel, L0_xattn_D, 8)
    x = x + jnp.tanh(g_ffn[0]) * _L0_ffn_ref(_layernorm(x, axis=-1), L0_ffn_W1, L0_ffn_B1, L0_ffn_W2, L0_ffn_B2, L0_ffn_LN_G, L0_ffn_LN_B)
    return x

_drawn_inputs = setup_inputs


def setup_inputs(seed=0):
    import zlib

    import numpy as np

    out = dict(_drawn_inputs(seed))
    spreads = {'L0_ffn_B1': (0.0, 0.8),
     'L0_ffn_B2': (0.0, 0.8),
     'L0_ffn_LN_G': (1.0, 0.6),
     'L0_ffn_LN_B': (0.0, 0.8)}
    factors = {'L0_ffn_W1': 4.605, 'L0_ffn_W2': 4.52}
    for name, (base, spread) in spreads.items():
        noise = np.random.default_rng([zlib.crc32(name.encode()), seed]).standard_normal(out[name].shape)
        drawn = base * np.exp(spread * noise) if base else spread * noise
        out[name] = jnp.asarray(drawn.astype(out[name].dtype))
    for name, factor in factors.items():
        out[name] = (out[name] * factor).astype(out[name].dtype)
    return out
```

```python
from contextlib import ExitStack

import concourse.bass as bass
from concourse import mybir

P = 128
F32 = mybir.dt.float32
F32R = mybir.dt.float32r
ALU = mybir.AluOpType
ACT = mybir.ActivationFunctionType
AX_X = mybir.AxisListType.X


def free_view(tensor, offset, dims):
    whole = tensor[:]
    return bass.AP(tensor=whole.tensor, offset=whole.offset + offset, ap=[list(whole.ap[0])] + dims)


def flat(ap):
    return ap.rearrange("a p n -> p (a n)")


def flat_free(ap):
    return ap.rearrange("p a n -> p (a n)")


def mixer_mlp_kernel(nc, x, ctx_in, gates, taps, skip, weights, bias1, bias2, gamma, beta, out):
    NT, _, D = x.shape
    NL, NH = weights.shape[0], weights.shape[1]
    HEADS = taps.shape[0]
    LC = D // P
    NB, R = 8, 8
    ND = 4
    PAIRS = ND * NB * R + NB * R // 2
    WRAP = R + ND
    TERMS, SPAN = 2 * ND, R + ND - 1
    NG, GT = 4, NT // 4
    EPS = 1e-5
    PAD = P
    RESIDENT = NH // 2
    PIECES = ((0, 3), (1, 2))
    WSLOTS = 4

    y1_dram = nc.dram_tensor("mixed_scratch", (NT, P, D), F32, kind="Internal").ap()
    taps_dram = nc.dram_tensor("padded_taps_scratch", (HEADS, PAD + D), F32, kind="Internal").ap()

    with ExitStack() as ctx:
        def sb(name, shape, dt=F32, scope=ctx):
            return scope.enter_context(nc.sbuf_tensor(name, shape, dt))

        def sem(name):
            return ctx.enter_context(nc.semaphore(name))

        w1_hi, w1_lo, w2_hi, w2_lo = ([None] * NH for _ in range(4))
        early = {}

        def hold_weights(lo, hi, scope, tag):
            for name, table in (("w1_hi", w1_hi), ("w1_lo", w1_lo), ("w2_hi", w2_hi), ("w2_lo", w2_lo)):
                part = sb(f"{name}_{tag}", [P, hi - lo, D], F32R, scope)
                early.setdefault(id(table), part)
                for t in range(lo, hi):
                    table[t] = part[:, t - lo, :]

        def half_tile(table, t):
            return flat_free(early[id(table)][:, bass.ds(t, 1), :])

        hold_weights(0, RESIDENT, ctx, "a")
        xres = sb("xres", [P, NT, D])
        wstage = sb("wstage", [P, WSLOTS, D])
        ident = sb("ident", [P, P])
        b1 = sb("b1", [P, NL * NH])
        gate = sb("gate", [P, 2])
        gate_tanh = sb("gate_tanh", [P, 2])
        half_power = sb("half_power", [P, GT])

        dma_const = sem("dma_const")
        dma_taps_in = sem("dma_taps_in")
        dma_taps_out = sem("dma_taps_out")
        dma_x = [sem(f"dma_x{i}") for i in range(2)]
        dma_c = [sem(f"dma_c{i}") for i in range(2)]
        dma_g = [sem(f"dma_g{i}") for i in range(2)]
        dma_wa = [sem(f"dma_wa{i}") for i in range(2)]
        dma_w = [sem(f"dma_w{i}") for i in range(WSLOTS)]
        dma_y1 = [sem(f"dma_y1_{i}") for i in range(2)]
        dma_vec = sem("dma_vec")
        dma_base = sem("dma_base")
        dma_out = sem("dma_out")
        ident_ready = sem("ident_ready")
        const_ready = sem("const_ready")
        wait_taken = sem("wait_taken")
        tanh_ready = sem("tanh_ready")
        taps_zero = sem("taps_zero")
        taps_ready = sem("taps_ready")
        dve_chain = sem("dve_chain")
        pool_chain = sem("pool_chain")
        stats1 = sem("stats1")
        rstd1 = sem("rstd1")
        qn_ready = sem("qn_ready")
        in_turned = sem("in_turned")
        qT_ready = sem("qT_ready")
        cT_ready = sem("cT_ready")
        pf_ready = sem("pf_ready")
        ph_ready = sem("ph_ready")
        pairs_ready = sem("pairs_ready")
        gh_ready = sem("gh_ready")
        g_ready = sem("g_ready")
        conv_done = sem("conv_done")
        y_used = sem("y_used")
        mix_ready = sem("mix_ready")
        out_turned = sem("out_turned")
        y1_ready = sem("y1_ready")
        stats2 = sem("stats2")
        rstd2 = sem("rstd2")
        x_ready = sem("x_ready")
        w_hi_ready = sem("w_hi_ready")
        w_ready = sem("w_ready")
        x_turned = sem("x_turned")
        xT_hi_ready = sem("xT_hi_ready")
        xT_ready = sem("xT_ready")
        mm1_done = sem("mm1_done")
        gelu_done = sem("gelu_done")
        h_ready = sem("h_ready")
        mm2_done = sem("mm2_done")
        biased = sem("biased")
        acc_free = sem("acc_free")
        sumsq = sem("sumsq")
        stats3 = sem("stats3")
        scaled = sem("scaled")
        fin_ready = sem("fin_ready")

        def standalone(eng):
            eng.sem_inc(wait_taken, 1)

        MM2 = NH - 1 + GT

        def rstd_chain(pool, link, mean, var, ve, tmp, rstd, nmr):
            standalone(pool)
            link(pool.tensor_scalar(ve, var, EPS, None, ALU.add))
            link(pool.tensor_tensor(rstd, ve, half_power[:, 0:ve.shape[-1]], ALU.pow))
            link(pool.tensor_tensor(tmp, rstd, rstd, ALU.mult))
            link(pool.tensor_tensor(tmp, tmp, ve, ALU.mult))
            standalone(pool)
            link(pool.tensor_scalar(tmp, tmp, -0.5, 1.5, ALU.mult, ALU.add))
            link(pool.tensor_tensor(rstd, rstd, tmp, ALU.mult))
            link(pool.tensor_tensor(tmp, mean, rstd, ALU.mult))
            standalone(pool)
            return pool.tensor_scalar(nmr, tmp, -1.0, None, ALU.mult)

        CH = 7

        def linker(eng, chain, base):
            n = [0]

            def link(ins):
                n[0] += 1
                ins.then_inc(chain, 1)
                eng.wait_ge(chain, base + n[0])
            return link, n

        with ExitStack() as scope:
            taps_sb = sb("taps_sb", [HEADS, PAD + D], F32, scope)
            skip_sb = sb("skip_sb", [HEADS, 1], F32, scope)
            xa = sb("xa", [P, 2, D], F32, scope)
            ca = sb("ca", [P, 2, D], F32, scope)
            qn = sb("qn", [P, D], F32, scope)
            qT = sb("qT", [P, 2, LC, 2, NB, WRAP], F32, scope)
            cT = sb("cT", [P, LC, 2, NB, WRAP], F32, scope)
            pf = sb("pf", [P, LC, PAIRS], F32, scope)
            ph = sb("ph", [P, 2, LC, PAIRS], F32R, scope)
            pl = sb("pl", [P, 2, LC, PAIRS], F32R, scope)
            graw = sb("graw", [P, 2, D], F32, scope)
            gh = sb("gh", [P, 2, D], F32R, scope)
            gl = sb("gl", [P, 2, D], F32R, scope)
            prod = sb("prod", [P, TERMS, 2, NB, SPAN], F32, scope)
            summed = sb("summed", [P, 2, NB, SPAN], F32, scope)
            mixT = sb("mixT", [P, 2, LC, P], F32, scope)
            y1 = sb("y1", [P, 2, D], F32, scope)
            st1 = sb("st1", [P, 6], F32, scope)
            mv1 = sb("mv1", [P, 2], F32, scope)
            ln1 = sb("ln1", [P, 4], F32, scope)
            st2 = sb("st2", [P, 6], F32, scope)
            mv2 = sb("mv2", [P, 2], F32, scope)
            ln2 = sb("ln2", [P, 4], F32, scope)
            ps_y = scope.enter_context(nc.psum_tensor("ps_y", [P, 4, 512], F32))
            ps_q = scope.enter_context(nc.psum_tensor("ps_q", [P, LC, P], F32))
            ps_c = scope.enter_context(nc.psum_tensor("ps_c", [P, LC, P], F32))
            ps_o = scope.enter_context(nc.psum_tensor("ps_o", [P, LC * P], F32))

            def toeplitz(head):
                first = taps_dram[bass.ds(head, 1), 1:1 + P]
                return bass.AP(tensor=first.tensor, offset=first.offset, ap=[[1, P], [1, D]])

            block = scope.enter_context(nc.Block())

            @block.sync
            def _(sp):
                sp.dma_start(taps_sb[:, PAD:], taps).then_inc(dma_taps_in, 16)
                sp.dma_start(skip_sb[:], skip).then_inc(dma_taps_in, 16)
                for k in range(2):
                    sp.dma_start(xa[:, k, :], x[k]).then_inc(dma_x[k], 16)
                    sp.dma_start(ca[:, k, :], ctx_in[k]).then_inc(dma_c[k], 16)
                sp.dma_start(gate[:], bass.AP(tensor=gates.tensor, offset=0, ap=[[0, P], [1, 2]])).then_inc(dma_const, 16)
                sp.dma_start(b1[:], bias1).then_inc(dma_const, 16)
                sp.wait_ge(taps_ready, 1)
                sp.dma_start(taps_dram, taps_sb[:]).then_inc(dma_taps_out, 16)
                sp.wait_ge(dma_taps_out, 16)
                for h in range(2):
                    sp.dma_start(graw[:, h, :], toeplitz(h)).then_inc(dma_g[h], 16)
                for k in range(2):
                    sp.dma_start(wstage[:, k, :], weights[0, 0, k]).then_inc(dma_wa[k], 16)
                    sp.sem_inc(dma_y1[k], 16)

                def tile(i, k, toeplitz_ahead, tiles_ahead):
                    T = 2 * i + k
                    if toeplitz_ahead:
                        for h in range(2):
                            sp.wait_ge(g_ready, 2 * T + h + 1)
                            sp.dma_start(graw[:, h, :], toeplitz(2 * T + 2 + h)).then_inc(dma_g[h], 16)
                    if tiles_ahead:
                        sp.wait_ge(w_ready, T + 1)
                        sp.dma_start(wstage[:, k, :], flat(weights[0, bass.ds(i + 1, 1), k])).then_inc(dma_wa[k], 16)
                    sp.wait_ge(y1_ready, T + 1)
                    if tiles_ahead:
                        sp.dma_start(xa[:, k, :], flat(x[bass.ds(T + 2, 1)])).then_inc(dma_x[k], 16)
                        sp.dma_start(ca[:, k, :], flat(ctx_in[bass.ds(T + 2, 1)])).then_inc(dma_c[k], 16)
                    sp.dma_start(flat(y1_dram[bass.ds(T, 1)]), y1[:, k, :]).then_inc(dma_y1[k], 16)

                with sp.Fori(0, NT // 2 - 1) as i:
                    tile(i, 0, True, True)
                    tile(i, 1, True, True)
                tile(NT // 2 - 1, 0, True, False)
                tile(NT // 2 - 1, 1, False, False)
                for k in range(2):
                    sp.wait_ge(dma_y1[k], 16 * (NT // 2 + 1))

            @block.tensor
            def _(pe):
                def turn_in(i, k, T, first=False):
                    if not first:
                        pe.wait_ge(cT_ready, T)
                    pe.wait_ge(dma_c[k], 16 * i + 16)
                    for c in range(LC):
                        pe.transpose(ps_c[:, c, :], ca[:, k, c * P:(c + 1) * P], ident[:])
                    pe.wait_ge(qn_ready, T + 1)
                    for c in range(LC):
                        last = pe.transpose(ps_q[:, c, :], qn[:, c * P:(c + 1) * P], ident[:])
                    last.then_inc(in_turned, 1)

                def conv(T, h, piece):
                    if piece == 0:
                        pe.wait_ge(pairs_ready, 2 * T + h + 1)
                        pe.wait_ge(g_ready, 2 * T + h + 1)
                    pe.wait_ge(y_used, 4 * T + 2 * h + piece + 1)
                    for s, lt in enumerate(PIECES[piece]):
                        ops = [(g, p, mt) for mt in range(lt + 1) for g, p in ((gh, ph), (gh, pl), (gl, ph))]
                        for a, (g, p, mt) in enumerate(ops):
                            last = pe.matmul(ps_y[:, 2 * piece + s, 0:PAIRS], g[:, h, (lt - mt) * P:(lt - mt + 1) * P],
                                             p[:, h, mt, :], start=(a == 0), stop=(a == len(ops) - 1))
                    last.then_inc(conv_done, 1)

                def turn_out(T, k):
                    pe.wait_ge(mix_ready, 4 * T + 4)
                    for c in range(LC):
                        last = pe.transpose(ps_o[:, c * P:(c + 1) * P], mixT[:, k, c, :], ident[:])
                    last.then_inc(out_turned, 1)

                def tile(i, k, ahead):
                    T = 2 * i + k
                    conv(T, 0, 1)
                    conv(T, 1, 0)
                    if ahead:
                        turn_in(i + k, 1 - k, T + 1)
                    conv(T, 1, 1)
                    turn_out(T, k)
                    if ahead:
                        conv(T + 1, 0, 0)

                pe.wait_ge(ident_ready, 1)
                turn_in(0, 0, 0, first=True)
                conv(0, 0, 0)
                with pe.Fori(0, NT // 2 - 1) as i:
                    tile(i, 0, True)
                    tile(i, 1, True)
                tile(NT // 2 - 1, 0, True)
                tile(NT // 2 - 1, 1, False)

            @block.scalar
            def _(act):
                def spread(T, k, first):
                    act.wait_ge(in_turned, T + 1)
                    if not first:
                        act.wait_ge(pf_ready, 2 * T)
                    for source, base, into in ((ps_c, 0, cT), (ps_q, k * LC * 2 * NB * WRAP, qT)):
                        for lo, n in ((0, R), (R, ND)):
                            last = act.activation(free_view(into, base + lo, [[WRAP, LC * 2 * NB], [1, n]]),
                                                  free_view(source, 0, [[R, LC * 2 * NB], [1, n]]), ACT.Copy)
                        last.then_inc(cT_ready if into is cT else qT_ready, 1)

                def head_hi(i, T, h, first):
                    if h == 1 and not first:
                        act.wait_ge(conv_done, 4 * T)
                    act.wait_ge(dma_g[h], 16 * T + 16)
                    act.activation(gh[:, h, :], graw[:, h, :], ACT.Copy).then_inc(gh_ready, 1)
                    act.wait_ge(pf_ready, 2 * T + h + 1)
                    act.activation(ph[:, h, :, :], pf[:], ACT.Copy).then_inc(ph_ready, 1)

                def tile(i, k, ahead):
                    T = 2 * i + k
                    if ahead:
                        spread(T + 1, 1 - k, False)
                        head_hi(i, T + 1, 0, False)
                        head_hi(i, T + 1, 1, False)
                    act.wait_ge(dma_wa[k], 16 * i + 16)
                    standalone(act)
                    act.activation(half_tile((w1_hi, w2_hi)[k], i), wstage[:, k, :], ACT.Copy).then_inc(w_hi_ready, 1)
                    act.wait_ge(rstd2, T + 1)
                    standalone(act)
                    act.activation(flat_free(xres[:, bass.ds(T, 1), :]), y1[:, k, :], ACT.Identity,
                                   bias=ln2[:, 3:4], scale=ln2[:, 2:3]).then_inc(x_ready, 1)

                act.wait_ge(dma_const, 32)
                act.activation(gate_tanh[:], gate[:], ACT.Tanh).then_inc(tanh_ready, 1)
                spread(0, 0, True)
                head_hi(0, 0, 0, True)
                head_hi(0, 0, 1, True)
                with act.Fori(0, NT // 2 - 1) as i:
                    tile(i, 0, True)
                    tile(i, 1, True)
                tile(NT // 2 - 1, 0, True)
                tile(NT // 2 - 1, 1, False)

            @block.gpsimd
            def _(pool):
                def head_pairs(T, h, first):
                    pool.wait_ge(cT_ready, T + 1)
                    if not first:
                        pool.wait_ge(pairs_ready, 2 * T + h)
                    for lt in range(LC):
                        at = (lt * 2 + h) * NB * WRAP
                        pool.tensor_tensor(free_view(pf, lt * PAIRS, [[NB * R, ND], [R, NB], [1, R]]),
                                           free_view(cT, at, [[0, ND], [WRAP, NB], [1, R]]),
                                           free_view(cT, at, [[1, ND], [WRAP, NB], [1, R]]), ALU.mult)
                    at = h * NB * WRAP
                    pool.tensor_tensor(free_view(pf, ND * NB * R, [[PAIRS, LC], [R // 2, NB], [1, R // 2]]),
                                       free_view(cT, at, [[2 * NB * WRAP, LC], [WRAP, NB], [1, R // 2]]),
                                       free_view(cT, at + ND, [[2 * NB * WRAP, LC], [WRAP, NB], [1, R // 2]]),
                                       ALU.mult).then_inc(pf_ready, 1)

                def toeplitz_lo(T, h):
                    pool.wait_ge(gh_ready, 2 * T + h + 1)
                    pool.tensor_tensor(gl[:, h, :], graw[:, h, :], gh[:, h, :].bitcast(F32),
                                       ALU.subtract).then_inc(g_ready, 1)

                def tile(i, k, ahead):
                    T = 2 * i + k
                    link, n = linker(pool, pool_chain, CH + 2 * CH * T)
                    if ahead:
                        pool.wait_ge(stats1, T + 2)
                        rstd_chain(pool, link, mv1[:, 0:1], mv1[:, 1:2], ln1[:, 0:1], ln1[:, 1:2], ln1[:, 2:3],
                                   ln1[:, 3:4]).then_inc(rstd1, 1)
                        head_pairs(T + 1, 0, False)
                        toeplitz_lo(T + 1, 0)
                        head_pairs(T + 1, 1, False)
                        toeplitz_lo(T + 1, 1)
                    else:
                        for _ in range(CH):
                            link(pool.memset(ln1[:, 0:1], 0.0))
                        pool.wait_ge(x_ready, T)
                    pool.wait_ge(stats2, T + 1)
                    rstd_chain(pool, link, mv2[:, 0:1], mv2[:, 1:2], ln2[:, 0:1], ln2[:, 1:2], ln2[:, 2:3],
                               ln2[:, 3:4]).then_inc(rstd2, 1)
                    assert n[0] == 2 * CH
                    pool.wait_ge(w_hi_ready, T + 1)
                    pool.tensor_tensor(half_tile((w1_lo, w2_lo)[k], i), wstage[:, k, :],
                                       half_tile((w1_hi, w2_hi)[k], i).bitcast(F32), ALU.subtract).then_inc(w_ready, 1)

                pool.memset(taps_sb[:, 0:PAD], 0.0).then_inc(taps_zero, 1)
                pool.memset(half_power[:], -0.5).then_inc(const_ready, 1)
                pool.memset(ident[:], 0.0).then_inc(const_ready, 1)
                pool.wait_ge(const_ready, 2)
                pool.affine_select(out=ident[:], in_=ident[:], compare_op=ALU.not_equal, fill=1.0, base=0,
                                   pattern=[[-1, P]], channel_multiplier=1).then_inc(ident_ready, 1)
                link, n = linker(pool, pool_chain, 0)
                pool.wait_ge(stats1, 1)
                rstd_chain(pool, link, mv1[:, 0:1], mv1[:, 1:2], ln1[:, 0:1], ln1[:, 1:2], ln1[:, 2:3],
                           ln1[:, 3:4]).then_inc(rstd1, 1)
                head_pairs(0, 0, True)
                toeplitz_lo(0, 0)
                head_pairs(0, 1, False)
                toeplitz_lo(0, 1)
                with pool.Fori(0, NT // 2 - 1) as i:
                    tile(i, 0, True)
                    tile(i, 1, True)
                tile(NT // 2 - 1, 0, True)
                tile(NT // 2 - 1, 1, False)

            @block.vector
            def _(dve):
                def input_stats(link, i, k):
                    dve.wait_ge(dma_x[k], 16 * i + 16)
                    link(dve.bn_stats(st1[:], xa[:, k, :]))
                    standalone(dve)
                    dve.bn_aggr(mv1[:], st1[:]).then_inc(stats1, 1)

                def normalise(T, k):
                    dve.wait_ge(rstd1, T + 1)
                    dve.tensor_scalar(qn[:], xa[:, k, :], mv1[:, 0:1], ln1[:, 2:3], ALU.subtract,
                                      ALU.mult).then_inc(qn_ready, 1)

                def pairs_lo(T, h):
                    dve.wait_ge(ph_ready, 2 * T + h + 1)
                    dve.tensor_tensor(pl[:, h, :, :], pf[:], ph[:, h, :, :].bitcast(F32),
                                      ALU.subtract).then_inc(pairs_ready, 1)

                def mix(link, T, k, h, piece):
                    n = 4 * T + 2 * h + piece
                    if h == 0 and piece == 0:
                        dve.wait_ge(qT_ready, T + 1)
                    dve.wait_ge(conv_done, n + 1)
                    row = 2 * NB * SPAN
                    for s, lt in enumerate(PIECES[piece]):
                        y_at = (2 * piece + s) * 512
                        q_at = ((k * LC + lt) * 2 + h) * NB * WRAP
                        p_at = s * NB * SPAN
                        dve.tensor_tensor(free_view(prod, p_at, [[row, ND], [SPAN, NB], [1, R]]),
                                          free_view(ps_y, y_at, [[NB * R, ND], [R, NB], [1, R]]),
                                          free_view(qT, q_at, [[1, ND], [WRAP, NB], [1, R]]), ALU.mult)
                        dve.tensor_tensor(free_view(prod, p_at + (ND + 1) * row + 1, [[row + 1, ND - 1], [SPAN, NB], [1, R]]),
                                          free_view(ps_y, y_at + NB * R, [[NB * R, ND - 1], [R, NB], [1, R]]),
                                          free_view(qT, q_at, [[0, ND - 1], [WRAP, NB], [1, R]]), ALU.mult)
                        last = dve.tensor_tensor(free_view(prod, p_at + ND * row, [[SPAN, NB], [R // 2, 2], [1, R // 2]]),
                                                 free_view(ps_y, y_at + ND * NB * R, [[R // 2, NB], [0, 2], [1, R // 2]]),
                                                 free_view(qT, q_at + ND, [[WRAP, NB], [R // 2, 2], [1, R // 2]]), ALU.mult)
                    last.then_inc(y_used, 1)
                    dve.wait_ge(y_used, n + 3)
                    link(dve.tensor_reduce(free_view(summed, 0, [[1, row]]), free_view(prod, 0, [[1, row], [row, TERMS]]),
                                           AX_X, ALU.add))
                    lt0, lt1 = PIECES[piece]
                    m_at = (k * LC + lt0) * P + h * NB * R
                    m_step = (lt1 - lt0) * P
                    over = SPAN - R
                    dve.tensor_tensor(free_view(mixT, m_at, [[m_step, 2], [R, NB], [1, over]]),
                                      free_view(summed, 0, [[NB * SPAN, 2], [SPAN, NB], [1, over]]),
                                      free_view(summed, R, [[NB * SPAN, 2], [SPAN, NB], [1, over]]), ALU.add)
                    dve.tensor_copy(free_view(mixT, m_at + over, [[m_step, 2], [R, NB], [1, R - over]]),
                                    free_view(summed, over, [[NB * SPAN, 2], [SPAN, NB], [1, R - over]])
                                    ).then_inc(mix_ready, 1)

                def add_gated(link, i, k):
                    T = 2 * i + k
                    dve.wait_ge(out_turned, T + 1)
                    dve.wait_ge(dma_y1[k], 16 * i + 16)
                    dve.scalar_tensor_tensor(out=y1[:, k, :], in0=ps_o[:], scalar=gate_tanh[:, 0:1], in1=xa[:, k, :],
                                             op0=ALU.mult, op1=ALU.add).then_inc(y1_ready, 1)
                    dve.wait_ge(y1_ready, T + 1)
                    link(dve.bn_stats(st2[:], y1[:, k, :]))
                    standalone(dve)
                    dve.bn_aggr(mv2[:], st2[:]).then_inc(stats2, 1)

                def tile(i, k, ahead, before):
                    T = 2 * i + k
                    link, n = linker(dve, dve_chain, before + 6 * T)
                    mix(link, T, k, 0, 1)
                    if ahead:
                        input_stats(link, i + k, 1 - k)
                    mix(link, T, k, 1, 0)
                    if ahead:
                        normalise(T + 1, 1 - k)
                    mix(link, T, k, 1, 1)
                    if ahead:
                        pairs_lo(T + 1, 0)
                    else:
                        dve.wait_ge(rstd2, T)
                    add_gated(link, i, k)
                    if ahead:
                        mix(link, T + 1, 1 - k, 0, 0)
                        pairs_lo(T + 1, 1)
                        assert n[0] == 6

                dve.wait_ge(dma_taps_in, 32)
                dve.wait_ge(taps_zero, 1)
                dve.tensor_tensor(taps_sb[:, PAD:PAD + 1], taps_sb[:, PAD:PAD + 1], skip_sb[:], ALU.add
                                  ).then_inc(taps_ready, 1)
                dve.memset(prod[:], 0.0).then_inc(y_used, 2)
                link, n = linker(dve, dve_chain, 0)
                dve.wait_ge(y_used, 2)
                input_stats(link, 0, 0)
                normalise(0, 0)
                pairs_lo(0, 0)
                dve.wait_ge(tanh_ready, 1)
                mix(link, 0, 0, 0, 0)
                pairs_lo(0, 1)
                before = n[0]
                with dve.Fori(0, NT // 2 - 1) as i:
                    tile(i, 0, True, before)
                    tile(i, 1, True, before)
                tile(NT // 2 - 1, 0, True, before)
                tile(NT // 2 - 1, 1, False, before)

        with ExitStack() as scope:
            hold_weights(RESIDENT, NH, scope, "b")
            xT_hi = sb("xT_hi", [P, LC, 512], F32R, scope)
            xT_lo = sb("xT_lo", [P, LC, 512], F32R, scope)
            h_full = sb("h_full", [P, 2, 512], F32, scope)
            h_hi = sb("h_hi", [P, 2, 512], F32R, scope)
            h_lo = sb("h_lo", [P, 2, 512], F32R, scope)
            vec = sb("vec", [P, 3, D], F32, scope)
            st3 = sb("st3", [P, GT, 6], F32, scope)
            mv3 = sb("mv3", [P, GT, 2], F32, scope)
            ln3 = sb("ln3", [P, 4, GT], F32, scope)
            acc = scope.enter_context(nc.psum_tensor("acc", [P, GT, 512], F32))
            ps_h = scope.enter_context(nc.psum_tensor("ps_h", [P, 2, 512], F32))
            ps_t = scope.enter_context(nc.psum_tensor("ps_t", [P, 2, 512], F32))
            block = scope.enter_context(nc.Block())
            HALVES = 2 * NH
            EARLY = 2 * RESIDENT

            def stage_value(layer, s):
                if isinstance(layer, int) and layer == 0:
                    return 16 * ((s - EARLY) // WSLOTS + 1)
                return 16 * ((HALVES - EARLY) // WSLOTS + (HALVES // WSLOTS) * (layer - 1) + s // WSLOTS + 1)

            @block.sync
            def _(sp):
                def load_vectors(L, norm):
                    sp.dma_start(vec[:, 0, :], across(bias2, L)).then_inc(dma_vec, 16)
                    if norm:
                        sp.dma_start(vec[:, 1, :], across(gamma, L)).then_inc(dma_vec, 16)
                        sp.dma_start(vec[:, 2, :], across(beta, L)).then_inc(dma_vec, 16)

                def across(table, L):
                    row = table[bass.ds(L, 1)]
                    return bass.AP(tensor=row.tensor, offset=row.offset, ap=[[0, P], [1, D]])

                def load_half(L, s, wait):
                    if wait:
                        sp.wait_ge(w_ready, HALVES * L + s - WSLOTS + 1)
                    sp.dma_start(wstage[:, s % WSLOTS, :], flat(weights[bass.ds(L, 1), s // 2, s % 2])
                                 ).then_inc(dma_w[s % WSLOTS], 16)

                for s in range(EARLY, HALVES):
                    load_half(0, s, s - EARLY >= WSLOTS)
                    if s == EARLY + 2:
                        load_vectors(0, True)

                def layer(L, last_norm):
                    for s in range(HALVES):
                        load_half(L + 1, s, True)
                    sp.wait_ge(x_ready, NT * (L + 2))
                    load_vectors(L + 1, not last_norm)

                with sp.Fori(0, NL - 2) as L:
                    layer(L, False)
                layer(NL - 2, True)
                sp.wait_ge(w_ready, HALVES * NL)
                for g in range(NG):
                    if g:
                        sp.wait_ge(fin_ready, GT * g)
                    sp.dma_start(wstage[:, :, :], y1_dram[GT * g:GT * g + GT].rearrange("t p d -> p t d")
                                 ).then_inc(dma_base, 16)
                    sp.wait_ge(fin_ready, GT * g + GT)
                    sp.dma_start(out[GT * g:GT * g + GT].rearrange("t p d -> p t d"), xres[:, GT * g:GT * g + GT, :]
                                 ).then_inc(dma_out, 16)
                sp.wait_ge(dma_out, 16 * NG)

            @block.tensor
            def _(pe):
                def turn(n, g, c):
                    if c == 0:
                        pe.wait_ge(x_ready, GT * n + GT)
                    elif c >= 2:
                        pe.wait_ge(xT_ready, LC * n + c - 1)
                    for j in range(GT):
                        last = pe.transpose(ps_t[:, c % 2, j * P:(j + 1) * P], xres[:, GT * g + j, c * P:(c + 1) * P],
                                            ident[:])
                    last.then_inc(x_turned, 1)

                def up(L, n, g, t):
                    if g == 0:
                        pe.wait_ge(w_ready, HALVES * L + 2 * t + 1)
                    for c in range(LC):
                        if t == 0:
                            pe.wait_ge(xT_ready, LC * n + c + 1)
                        cs = slice(c * P, (c + 1) * P)
                        pe.matmul(ps_h[:, t % 2, :], w1_hi[t][:, cs], xT_hi[:, c, :], start=(c == 0), stop=False)
                        pe.matmul(ps_h[:, t % 2, :], w1_hi[t][:, cs], xT_lo[:, c, :], start=False, stop=False)
                        last = pe.matmul(ps_h[:, t % 2, :], w1_lo[t][:, cs], xT_hi[:, c, :], start=False,
                                         stop=(c == LC - 1))
                    last.then_inc(mm1_done, 1)

                def down(L, n, g, t, tiles):
                    if g == 0:
                        pe.wait_ge(w_ready, HALVES * L + 2 * t + 2)
                    pe.wait_ge(h_ready, NH * n + t + 1)
                    for j in tiles:
                        if t == 0:
                            pe.wait_ge(acc_free, GT * n + j + 1)
                        js = slice(j * P, (j + 1) * P)
                        pe.matmul(acc[:, j, :], h_hi[:, t % 2, js], w2_hi[t], start=(t == 0), stop=False)
                        pe.matmul(acc[:, j, :], h_hi[:, t % 2, js], w2_lo[t], start=False, stop=False)
                        last = pe.matmul(acc[:, j, :], h_lo[:, t % 2, js], w2_hi[t], start=False, stop=(t == NH - 1))
                        if t == NH - 1:
                            last.then_inc(mm2_done, 1)
                    if t < NH - 1:
                        last.then_inc(mm2_done, 1)

                def group(L, g, more):
                    n = NG * L + g
                    for t in range(NH):
                        up(L, n, g, t)
                        if t:
                            down(L, n, g, t - 1, range(GT))
                    if more:
                        g2 = (g + 1) % NG
                        turn(n + 1, g2, 0)
                        turn(n + 1, g2, 1)
                        down(L, n, g, NH - 1, [0, 1])
                        turn(n + 1, g2, 2)
                        down(L, n, g, NH - 1, [2])
                        turn(n + 1, g2, 3)
                        down(L, n, g, NH - 1, [3])
                    else:
                        down(L, n, g, NH - 1, range(GT))

                for c in range(LC):
                    turn(0, 0, c)
                with pe.Fori(0, NL - 1) as L:
                    for g in range(NG):
                        group(L, g, True)
                for g in range(NG):
                    group(NL - 1, g, g < NG - 1)

            @block.scalar
            def _(act):
                def weight_hi(L, t):
                    for half, table in ((0, w1_hi), (1, w2_hi)):
                        s = 2 * t + half
                        act.wait_ge(dma_w[s % WSLOTS], stage_value(L, s))
                        act.activation(table[t], wstage[:, s % WSLOTS, :], ACT.Copy).then_inc(w_hi_ready, 1)

                def input_hi(n, c):
                    act.wait_ge(x_turned, LC * n + c + 1)
                    act.activation(xT_hi[:, c, :], ps_t[:, c % 2, :], ACT.Copy).then_inc(xT_hi_ready, 1)

                def group(L, g, more, reload):
                    n = NG * L + g
                    for t in range(NH):
                        act.wait_ge(mm1_done, NH * n + t + 1)
                        bias = b1[:, bass.ds(NH * L + t, 1)]
                        standalone(act)
                        act.activation(h_hi[:, t % 2, :], ps_h[:, t % 2, :], ACT.Gelu, bias=bias)
                        act.activation(h_full[:, t % 2, :], ps_h[:, t % 2, :], ACT.Gelu, bias=bias).then_inc(gelu_done, 1)
                        if reload and t >= 2:
                            weight_hi(L + 1, t - 2)
                    if more:
                        for c in range(LC):
                            input_hi(n + 1, c)
                    if reload:
                        act.wait_ge(mm2_done, MM2 * n + NH - 1)
                        weight_hi(L + 1, NH - 2)
                        act.wait_ge(mm2_done, MM2 * n + MM2)
                        weight_hi(L + 1, NH - 1)

                for c in range(LC):
                    input_hi(0, c)
                for t in range(RESIDENT, NH):
                    weight_hi(0, t)
                with act.Fori(0, NL - 1) as L:
                    for g in range(NG):
                        group(L, g, True, g == NG - 1)
                for g in range(NG):
                    group(NL - 1, g, g < NG - 1, False)

            @block.vector
            def _(dve):
                def weight_lo(L, t):
                    for half, hi, lo in ((0, w1_hi, w1_lo), (1, w2_hi, w2_lo)):
                        s = 2 * t + half
                        dve.wait_ge(w_hi_ready, HALVES * L + s + 1)
                        dve.tensor_tensor(lo[t], wstage[:, s % WSLOTS, :], hi[t].bitcast(F32), ALU.subtract
                                          ).then_inc(w_ready, 1)

                def input_lo(n, c):
                    dve.wait_ge(xT_hi_ready, LC * n + c + 1)
                    dve.tensor_tensor(xT_lo[:, c, :], ps_t[:, c % 2, :], xT_hi[:, c, :].bitcast(F32), ALU.subtract
                                      ).then_inc(xT_ready, 1)

                def read_out(n, g, j):
                    dve.wait_ge(mm2_done, MM2 * n + NH - 1 + j + 1)
                    dve.wait_ge(biased, GT * n + j + 1)
                    dve.tensor_tensor(xres[:, GT * g + j, :], acc[:, j, :], xres[:, GT * g + j, :], ALU.add
                                      ).then_inc(acc_free, 1)

                def tile_stats(n, g, j):
                    dve.wait_ge(acc_free, GT * (n + 1) + j + 1)
                    dve.bn_stats(st3[:, j, :], xres[:, GT * g + j, :]).then_inc(sumsq, 1)

                def finish(n, g, j):
                    dve.wait_ge(acc_free, GT * (n + 1) + j + 1)
                    if j == 0:
                        dve.wait_ge(dma_base, 16 * (g + 1))
                    dve.scalar_tensor_tensor(out=xres[:, GT * g + j, :], in0=xres[:, GT * g + j, :],
                                             scalar=gate_tanh[:, 1:2], in1=wstage[:, j, :], op0=ALU.mult,
                                             op1=ALU.add).then_inc(fin_ready, 1)

                def group(L, g, more, reload, norm):
                    n = NG * L + g
                    for t in range(NH):
                        dve.wait_ge(gelu_done, NH * n + t + 1)
                        dve.tensor_tensor(h_lo[:, t % 2, :], h_full[:, t % 2, :], h_hi[:, t % 2, :].bitcast(F32),
                                          ALU.subtract).then_inc(h_ready, 1)
                        if reload and t >= 2:
                            weight_lo(L + 1, t - 2)
                    close = tile_stats if norm else finish
                    steps = [(input_lo, 0), (input_lo, 1), (read_out, 0), (input_lo, 2), (read_out, 1), (close, 0),
                             (input_lo, 3), (read_out, 2), (close, 1), (read_out, 3), (close, 2), (close, 3)]
                    for step, a in steps:
                        if step is input_lo:
                            if more:
                                input_lo(n + 1, a)
                        else:
                            step(n, g, a)
                    if norm:
                        dve.wait_ge(sumsq, GT * n + GT)
                        standalone(dve)
                        for j in range(GT):
                            last = dve.bn_aggr(mv3[:, j, :], st3[:, j, :])
                        last.then_inc(stats3, 1)
                    if reload:
                        weight_lo(L + 1, NH - 2)
                        weight_lo(L + 1, NH - 1)

                dve.sem_inc(acc_free, GT)
                for c in range(LC):
                    input_lo(0, c)
                for t in range(RESIDENT, NH):
                    weight_lo(0, t)
                with dve.Fori(0, NL - 1) as L:
                    for g in range(NG):
                        group(L, g, True, g == NG - 1, True)
                for g in range(NG):
                    group(NL - 1, g, g < NG - 1, False, False)

            @block.gpsimd
            def _(pool):
                base = CH + 2 * CH * NT
                per = CH + 2

                def group(L, g, norm):
                    n = NG * L + g
                    pool.wait_ge(x_turned, LC * n + LC)
                    if norm:
                        pool.wait_ge(dma_vec, 48 * L + 48)
                    else:
                        pool.wait_ge(dma_vec, 48 * L + 16)
                    for j in range(GT):
                        xj = xres[:, GT * g + j, :]
                        pool.tensor_tensor(xj, xj, vec[:, 0, :], ALU.add).then_inc(biased, 1)
                    if not norm:
                        return
                    link, k = linker(pool, pool_chain, base + per * n)
                    pool.wait_ge(stats3, n + 1)
                    rs, nm = ln3[:, 2, :], ln3[:, 3, :]
                    ln_done = rstd_chain(pool, link, mv3[:, :, 0], mv3[:, :, 1], ln3[:, 0, :], ln3[:, 1, :], rs, nm)
                    link(ln_done)
                    standalone(pool)
                    for j in range(GT):
                        xj = xres[:, GT * g + j, :]
                        last = pool.tensor_scalar(xj, xj, rs[:, j:j + 1], nm[:, j:j + 1], ALU.mult, ALU.add)
                    link(last)
                    for j in range(GT):
                        xj = xres[:, GT * g + j, :]
                        last = pool.tensor_tensor(xj, xj, vec[:, 1, :], ALU.mult)
                    last.then_inc(scaled, 1)
                    pool.wait_ge(scaled, n + 1)
                    for j in range(GT):
                        xj = xres[:, GT * g + j, :]
                        pool.tensor_tensor(xj, xj, vec[:, 2, :], ALU.add).then_inc(x_ready, 1)
                    assert k[0] == per

                with pool.Fori(0, NL - 1) as L:
                    for g in range(NG):
                        group(L, g, True)
                for g in range(NG):
                    group(NL - 1, g, False)


def kernel(**inputs):
    import numpy as _np
    import concourse.bacc as _bacc
    from concourse import mybir as _mybir
    from concourse.bass_utils import run_bass_kernel_spmd as _run

    a = {k: _np.asarray(v) for k, v in inputs.items()}
    x, c = a["x"], a["ctx_2048"]
    B, S, D = x.shape
    R, NT = 8, B * S // 128

    def tiles(m):
        return m.reshape(B, NT, 2, R, D).transpose(1, 2, 0, 3, 4).reshape(NT, 128, D)

    w1, w2 = a["L0_ffn_W1"], a["L0_ffn_W2"]
    NL, H, _ = w1.shape
    LC, NH = D // 128, H // 128
    w1t = w1.reshape(NL, NH, 128, LC, 128).transpose(0, 1, 4, 3, 2).reshape(NL, NH, 1, 128, D)
    w2t = w2.reshape(NL, D, NH, 128).transpose(0, 2, 3, 1).reshape(NL, NH, 1, 128, D)
    arrays = {
        "x": tiles(x),
        "ctx_in": tiles(c.reshape(B, S, LC, 128)[..., ::-1].reshape(B, S, D)),
        "gates": _np.concatenate([a["g_xattn"], a["g_ffn"]]),
        "taps": a["L0_xattn_ssm_kernel"],
        "skip": a["L0_xattn_D"].reshape(-1, 1),
        "weights": _np.concatenate([w1t, w2t], axis=2),
        "bias1": a["L0_ffn_B1"].reshape(NL, NH, 128).transpose(2, 0, 1).reshape(128, NL * NH),
        "bias2": a["L0_ffn_B2"],
        "gamma": a["L0_ffn_LN_G"],
        "beta": a["L0_ffn_LN_B"],
    }
    arrays = {k: _np.ascontiguousarray(v) for k, v in arrays.items()}
    nc = _bacc.Bacc("TRN2", target_bir_lowering=False, num_devices=1)
    args = [nc.dram_tensor(k, v.shape, _mybir.dt.float32, kind="ExternalInput").ap() for k, v in arrays.items()]
    args.append(nc.dram_tensor("mixed_out", (NT, 128, D), _mybir.dt.float32, kind="ExternalOutput").ap())
    mixer_mlp_kernel(nc, *args)
    r = _run(nc, [arrays], core_ids=[0])
    y = r.results[0]["mixed_out"]
    return y.reshape(NT, 2, B, R, D).transpose(2, 0, 1, 3, 4).reshape(B, S, D)
```

```python
from contextlib import ExitStack

import concourse.bass as bass
from concourse import mybir

P = 128
F32 = mybir.dt.float32
F32R = mybir.dt.float32r
ALU = mybir.AluOpType
ACT = mybir.ActivationFunctionType
AX_X = mybir.AxisListType.X


def free_view(tensor, offset, dims):
    whole = tensor[:]
    return bass.AP(tensor=whole.tensor, offset=whole.offset + offset, ap=[list(whole.ap[0])] + dims)


def flat(ap):
    return ap.rearrange("a p n -> p (a n)")


def flat_free(ap):
    return ap.rearrange("p a n -> p (a n)")


def mixer_mlp_kernel(nc, x, ctx_in, gates, taps, skip, weights, bias1, bias2, gamma, beta, out):
    NT, _, D = x.shape
    NL, NH = weights.shape[0], weights.shape[1]
    HEADS = taps.shape[0]
    LC = D // P
    NB, R = 8, 8
    ND = 4
    PAIRS = ND * NB * R + NB * R // 2
    WRAP = R + ND
    TERMS, SPAN = 2 * ND, R + ND - 1
    NG, GT = 4, NT // 4
    EPS = 1e-5
    PAD = P
    RESIDENT = 3 * NH // 4
    PIECES = ((0, 3), (1, 2))
    WSLOTS = 4
    CREDIT = 2

    y1_dram = nc.dram_tensor("mixed_scratch", (NT, P, D), F32, kind="Internal").ap()
    taps_dram = nc.dram_tensor("padded_taps_scratch", (HEADS, PAD + D), F32, kind="Internal").ap()

    with ExitStack() as ctx:
        def sb(name, shape, dt=F32, scope=ctx):
            return scope.enter_context(nc.sbuf_tensor(name, shape, dt))

        def sem(name):
            return ctx.enter_context(nc.semaphore(name))

        w1_hi, w1_lo, w2_hi, w2_lo = ([None] * NH for _ in range(4))
        early = {}

        def hold_weights(lo, hi, scope, tag):
            for name, table in (("w1_hi", w1_hi), ("w1_lo", w1_lo), ("w2_hi", w2_hi), ("w2_lo", w2_lo)):
                part = sb(f"{name}_{tag}", [P, hi - lo, D], F32R, scope)
                early.setdefault(id(table), part)
                for t in range(lo, hi):
                    table[t] = part[:, t - lo, :]

        def half_tile(table, t):
            return flat_free(early[id(table)][:, bass.ds(t, 1), :])

        hold_weights(0, RESIDENT, ctx, "a")
        xres = sb("xres", [P, NT, D])
        wstage = sb("wstage", [P, WSLOTS, D])
        ident = sb("ident", [P, P])
        b1 = sb("b1", [P, NL * NH])
        gate = sb("gate", [P, 2])
        gate_tanh = sb("gate_tanh", [P, 2])
        half_power = sb("half_power", [P, NT - GT])

        dma_const = sem("dma_const")
        dma_taps_in = sem("dma_taps_in")
        dma_taps_out = sem("dma_taps_out")
        dma_x = [sem(f"dma_x{i}") for i in range(4)]
        dma_c = [sem(f"dma_c{i}") for i in range(2)]
        dma_g = [sem(f"dma_g{i}") for i in range(2)]
        dma_wa = [sem(f"dma_wa{i}") for i in range(2)]
        dma_w = [sem(f"dma_w{i}") for i in range(WSLOTS)]
        dma_y1 = [sem(f"dma_y1_{i}") for i in range(4)]
        dma_vec = sem("dma_vec")
        dma_base = sem("dma_base")
        dma_out = sem("dma_out")
        ident_ready = sem("ident_ready")
        const_ready = sem("const_ready")
        wait_taken = sem("wait_taken")
        tanh_ready = sem("tanh_ready")
        taps_zero = sem("taps_zero")
        prod_zero = sem("prod_zero")
        taps_ready = sem("taps_ready")
        dve_chain = sem("dve_chain")
        pool_chain = sem("pool_chain")
        stats1 = sem("stats1")
        st1_ready = sem("st1_ready")
        terms_added = sem("terms_added")
        terms_summed = sem("terms_summed")
        mix_copied = sem("mix_copied")
        rstd1 = sem("rstd1")
        qn_ready = sem("qn_ready")
        in_turned = sem("in_turned")
        qT_ready = sem("qT_ready")
        cT_ready = sem("cT_ready")
        pairs_ready = sem("pairs_ready")
        conv_done = sem("conv_done")
        y_used = sem("y_used")
        mix_ready = sem("mix_ready")
        out_turned = sem("out_turned")
        y1_ready = sem("y1_ready")
        stats2 = sem("stats2")
        rstd2 = sem("rstd2")
        x_ready = sem("x_ready")
        w_hi_ready = sem("w_hi_ready")
        w_ready = sem("w_ready")
        x_turned = sem("x_turned")
        xT_hi_ready = sem("xT_hi_ready")
        xT_ready = sem("xT_ready")
        mm1_done = sem("mm1_done")
        gelu_done = sem("gelu_done")
        h_ready = sem("h_ready")
        mm2_done = sem("mm2_done")
        biased = sem("biased")
        acc_free = sem("acc_free")
        sumsq = sem("sumsq")
        stats3 = sem("stats3")
        scaled = sem("scaled")
        fin_ready = sem("fin_ready")

        def standalone(eng):
            eng.sem_inc(wait_taken, 1)

        MM2 = NH - 1 + GT

        def rstd_chain(pool, link, mean, var, ve, tmp, rstd, nmr):
            standalone(pool)
            link(pool.tensor_scalar(ve, var, EPS, None, ALU.add))
            link(pool.tensor_tensor(rstd, ve, half_power[:, 0:ve.shape[-1]], ALU.pow))
            link(pool.tensor_tensor(tmp, rstd, rstd, ALU.mult))
            link(pool.tensor_tensor(tmp, tmp, ve, ALU.mult))
            standalone(pool)
            link(pool.tensor_scalar(tmp, tmp, -0.5, 1.5, ALU.mult, ALU.add))
            link(pool.tensor_tensor(rstd, rstd, tmp, ALU.mult))
            link(pool.tensor_tensor(tmp, mean, rstd, ALU.mult))
            standalone(pool)
            return pool.tensor_scalar(nmr, tmp, -1.0, None, ALU.mult)

        CH = 7

        def linker(eng, chain, base):
            n = [0]

            def link(ins):
                n[0] += 1
                ins.then_inc(chain, 1)
                eng.wait_ge(chain, base + n[0])
            return link, n

        with ExitStack() as scope:
            taps_sb = sb("taps_sb", [HEADS, PAD + D], F32, scope)
            skip_sb = sb("skip_sb", [HEADS, 1], F32, scope)
            ca = sb("ca", [P, 2, D], F32, scope)
            qn = sb("qn", [P, 2, D], F32, scope)
            qT = sb("qT", [P, 2, LC, 2, NB, WRAP], F32, scope)
            cT = sb("cT", [P, LC, 2, NB, WRAP], F32, scope)
            pairs = sb("pairs", [P, 2, LC, PAIRS], F32, scope)
            lags = sb("lags", [P, 2, D], F32, scope)
            prod = sb("prod", [P, 2, TERMS, 2, NB, SPAN], F32, scope)
            summed = sb("summed", [P, 2, 2, NB, SPAN], F32, scope)
            mixT = sb("mixT", [P, 2, LC, P], F32, scope)
            st1 = sb("st1", [P, NT, 6], F32, scope)
            mv1 = sb("mv1", [P, NT, 2], F32, scope)
            ln1 = sb("ln1", [P, 4, NT], F32, scope)
            st2 = sb("st2", [P, GT, 6], F32, scope)
            mv2 = sb("mv2", [P, GT, 2], F32, scope)
            ln2 = sb("ln2", [P, 4, GT], F32, scope)
            ps_y = scope.enter_context(nc.psum_tensor("ps_y", [P, 4, 512], F32))
            ps_q = scope.enter_context(nc.psum_tensor("ps_q", [P, LC, P], F32))
            ps_c = scope.enter_context(nc.psum_tensor("ps_c", [P, LC, P], F32))
            ps_o = scope.enter_context(nc.psum_tensor("ps_o", [P, LC * P], F32))
            ps_s = scope.enter_context(nc.psum_tensor("ps_s", [P, 512], F32))

            ROW = 2 * NB * SPAN
            BUF = TERMS * ROW

            def toeplitz(head):
                first = taps_dram[bass.ds(head, 1), 1:1 + P]
                return bass.AP(tensor=first.tensor, offset=first.offset, ap=[[1, P], [1, D]])

            def xtile(T):
                return flat_free(xres[:, bass.ds(T, 1), :])

            HPG = 2 * RESIDENT * GT // NT

            def halves(k):
                return [divmod(m, 2) for m in range(HPG * k // GT, HPG * (k + 1) // GT)]

            def last_two(T):
                return isinstance(T, int) and T >= NT - 2

            def over_tiles(eng, tile):
                tile(0, 0, True, False)
                with eng.Fori(0, NT // GT - 1) as i:
                    for k in range(1, GT):
                        tile(i, k, True, False)
                    tile(i + 1, 0, True, True)
                for k in range(1, GT):
                    tile(NT // GT - 1, k, k < GT - 1, False)

            block = scope.enter_context(nc.Block())

            @block.sync
            def _(sp):
                sp.dma_start(taps_sb[:, PAD:], taps).then_inc(dma_taps_in, 16)
                sp.dma_start(skip_sb[:], skip).then_inc(dma_taps_in, 16)
                for g in range(NG):
                    sp.dma_start(xres[:, GT * g:GT * g + GT, :], x[GT * g:GT * g + GT].rearrange("t p d -> p t d")
                                 ).then_inc(dma_x[g], 16)
                    if g == 0:
                        for k in range(2):
                            sp.dma_start(ca[:, k, :], ctx_in[k]).then_inc(dma_c[k], 16)
                    if g == 1:
                        sp.wait_ge(taps_ready, 1)
                        sp.dma_start(taps_dram, taps_sb[:]).then_inc(dma_taps_out, 16)
                        sp.dma_start(gate[:], bass.AP(tensor=gates.tensor, offset=0, ap=[[0, P], [1, 2]])
                                     ).then_inc(dma_const, 16)
                        sp.dma_start(b1[:], bias1).then_inc(dma_const, 16)
                sp.wait_ge(dma_taps_out, 16)
                for h in range(2):
                    sp.dma_start(lags[:, h, :], toeplitz(h)).then_inc(dma_g[h], 16)

                def tile(i, k, ahead, _):
                    T = GT * i + k
                    if not last_two(T):
                        sp.wait_ge(in_turned, T + 1)
                        sp.dma_start(ca[:, k % 2, :], flat(ctx_in[bass.ds(T + 2, 1)])).then_inc(dma_c[k % 2], 16)
                    if ahead:
                        for h in range(2):
                            sp.wait_ge(conv_done, 4 * T + 2 * h + 2)
                            sp.dma_start(lags[:, h, :], toeplitz(2 * T + 2 + h)).then_inc(dma_g[h], 16)
                    for t, half in halves(k):
                        m = HPG * i + 2 * t + half
                        sp.wait_ge(w_ready, m + 1)
                        sp.dma_start(wstage[:, half, :],
                                     flat(weights[0, bass.ds(HPG // 2 * i + t, 1), half])
                                     ).then_inc(dma_wa[half], 16)
                    sp.wait_ge(y1_ready, T + 1)
                    sp.dma_start(flat(y1_dram[bass.ds(T, 1)]), xtile(T)).then_inc(dma_y1[k], 16)

                over_tiles(sp, tile)

            @block.tensor
            def _(pe):
                def turn_in(i, k, T, first=False):
                    if not first:
                        pe.wait_ge(qT_ready, T)
                    pe.wait_ge(dma_c[k % 2], 32 * i + 16 * (k // 2) + 16)
                    for c in range(LC):
                        pe.transpose(ps_c[:, c, :], ca[:, k % 2, c * P:(c + 1) * P], ident[:])
                    pe.wait_ge(qn_ready, T + 1)
                    for c in range(LC):
                        last = pe.transpose(ps_q[:, c, :], qn[:, k % 2, c * P:(c + 1) * P], ident[:])
                    last.then_inc(in_turned, 1)

                def conv(T, h, piece):
                    if piece == 0:
                        pe.wait_ge(pairs_ready, 2 * T + h + 1)
                        pe.wait_ge(dma_g[h], 16 * T + 16)
                    pe.wait_ge(y_used, 4 * T + 2 * h + piece + 1)
                    for s, lt in enumerate(PIECES[piece]):
                        for mt in range(lt + 1):
                            last = pe.matmul(ps_y[:, 2 * piece + s, 0:PAIRS],
                                             lags[:, h, (lt - mt) * P:(lt - mt + 1) * P], pairs[:, h, mt, :],
                                             start=(mt == 0), stop=(mt == lt))
                    last.then_inc(conv_done, 1)

                def add_terms(T, n_in_tile):
                    pe.wait_ge(y_used, 4 * T + n_in_tile + 3)
                    buf = (n_in_tile % 2) * BUF
                    for a in range(TERMS):
                        pe.matmul(ps_s[:, 0:2 * NB * R], ident[:], free_view(prod, buf + a * ROW, [[SPAN, 2 * NB], [1, R]]),
                                  start=(a == 0), stop=False, skip_group_check=True)
                    for d in range(1, ND):
                        last = pe.matmul(free_view(ps_s, 0, [[R, 2 * NB], [1, d]]), ident[:],
                                         free_view(prod, buf + (ND + d) * ROW + R, [[SPAN, 2 * NB], [1, d]]),
                                         start=False, stop=(d == ND - 1), skip_group_check=True)
                    last.then_inc(terms_added, 1)

                def turn_out(T, k):
                    pe.wait_ge(mix_ready, 3 * T + 3)
                    pe.wait_ge(mix_copied, T + 1)
                    for c in range(LC):
                        last = pe.transpose(ps_o[:, c * P:(c + 1) * P], mixT[:, k % 2, c, :], ident[:])
                    last.then_inc(out_turned, 1)

                def tile(i, k, ahead, _):
                    T = GT * i + k
                    conv(T, 0, 1)
                    conv(T, 1, 0)
                    conv(T, 1, 1)
                    if ahead:
                        conv(T + 1, 0, 0)
                    add_terms(T, 3)
                    if not last_two(T):
                        turn_in(i + (k + 2) // GT, (k + 2) % GT, T + 2)
                    turn_out(T, k)

                pe.wait_ge(ident_ready, 1)
                turn_in(0, 0, 0, first=True)
                turn_in(0, 1, 1)
                conv(0, 0, 0)
                over_tiles(pe, tile)

            @block.scalar
            def _(act):
                def normalise(T, k):
                    standalone(act)
                    act.activation(qn[:, k % 2, :], xtile(T), ACT.Identity, bias=ln1[:, 3, bass.ds(T, 1)],
                                   scale=ln1[:, 2, bass.ds(T, 1)]).then_inc(qn_ready, 1)

                def spread(T, k, first):
                    act.wait_ge(in_turned, T + 1)
                    if not first:
                        act.wait_ge(pairs_ready, 2 * T)
                    for source, base, into in ((ps_c, 0, cT), (ps_q, (k % 2) * LC * 2 * NB * WRAP, qT)):
                        for lo, n in ((0, R), (R, ND)):
                            last = act.activation(free_view(into, base + lo, [[WRAP, LC * 2 * NB], [1, n]]),
                                                  free_view(source, 0, [[R, LC * 2 * NB], [1, n]]), ACT.Copy)
                        last.then_inc(cT_ready if into is cT else qT_ready, 1)

                def second_norm(i):
                    act.wait_ge(rstd2, i + 1)
                    for k in range(GT):
                        act.wait_ge(dma_y1[k], 16 * i + 16)
                        standalone(act)
                        act.activation(xtile(GT * i + k), xtile(GT * i + k), ACT.Identity, bias=ln2[:, 3, k:k + 1],
                                       scale=ln2[:, 2, k:k + 1]).then_inc(x_ready, 1)

                def tile(i, k, ahead, group_done):
                    T = GT * i + k
                    act.wait_ge(terms_added, T + 1)
                    m_at = ((k % 2) * LC + PIECES[1][0]) * P + NB * R
                    m_step = (PIECES[1][1] - PIECES[1][0]) * P
                    act.activation(free_view(mixT, m_at, [[m_step, 2], [1, NB * R]]),
                                   free_view(ps_s, 0, [[NB * R, 2], [1, NB * R]]), ACT.Copy).then_inc(mix_copied, 1)
                    if not last_two(T):
                        spread(T + 2, k + 2, False)
                        if not (isinstance(T, int) and T >= NT - 3):
                            normalise(T + 3, k + 3)
                    for t, half in halves(k):
                        m = HPG * i + 2 * t + half
                        act.wait_ge(dma_wa[half], 16 * (HPG // 2 * i + t + 1))
                        standalone(act)
                        act.activation(half_tile((w1_hi, w2_hi)[half], HPG // 2 * i + t),
                                       wstage[:, half, :], ACT.Copy).then_inc(w_hi_ready, 1)
                    if group_done:
                        second_norm(i - 1)

                act.wait_ge(dma_const, 32)
                act.activation(gate_tanh[:], gate[:], ACT.Tanh).then_inc(tanh_ready, 1)
                act.wait_ge(rstd1, 1)
                normalise(0, 0)
                normalise(1, 1)
                spread(0, 0, True)
                normalise(2, 2)
                spread(1, 1, False)
                act.wait_ge(rstd1, 2)
                over_tiles(act, tile)
                second_norm(NT // GT - 1)

            @block.gpsimd
            def _(pool):
                def head_pairs(T, h, first):
                    pool.wait_ge(cT_ready, T + 1)
                    if not first:
                        pool.wait_ge(conv_done, 4 * T - 2 + 2 * h)
                    for lt in range(LC):
                        at = (lt * 2 + h) * NB * WRAP
                        pool.tensor_tensor(free_view(pairs, (h * LC + lt) * PAIRS, [[NB * R, ND], [R, NB], [1, R]]),
                                           free_view(cT, at, [[0, ND], [WRAP, NB], [1, R]]),
                                           free_view(cT, at, [[1, ND], [WRAP, NB], [1, R]]), ALU.mult)
                    at = h * NB * WRAP
                    pool.tensor_tensor(free_view(pairs, h * LC * PAIRS + ND * NB * R,
                                                 [[PAIRS, LC], [R // 2, NB], [1, R // 2]]),
                                       free_view(cT, at, [[2 * NB * WRAP, LC], [WRAP, NB], [1, R // 2]]),
                                       free_view(cT, at + ND, [[2 * NB * WRAP, LC], [WRAP, NB], [1, R // 2]]),
                                       ALU.mult).then_inc(pairs_ready, 1)

                def first_rstd(link, lo, hi):
                    rstd_chain(pool, link, mv1[:, lo:hi, 0], mv1[:, lo:hi, 1],
                               *[ln1[:, r, lo:hi] for r in range(4)]).then_inc(rstd1, 1)

                def second_rstd(i):
                    link, n = linker(pool, pool_chain, 2 * CH + CH * i)
                    pool.wait_ge(stats2, GT * i + GT)
                    rstd_chain(pool, link, mv2[:, :, 0], mv2[:, :, 1], *[ln2[:, r, :] for r in range(4)]
                               ).then_inc(rstd2, 1)
                    assert n[0] == CH

                def tile(i, k, ahead, group_done):
                    T = GT * i + k
                    if ahead:
                        head_pairs(T + 1, 0, False)
                    if group_done:
                        second_rstd(i - 1)
                    if ahead:
                        head_pairs(T + 1, 1, False)
                    for t, half in halves(k):
                        m = HPG * i + 2 * t + half
                        pool.wait_ge(w_hi_ready, m + 1)
                        pool.tensor_tensor(half_tile((w1_lo, w2_lo)[half], HPG // 2 * i + t),
                                           wstage[:, half, :],
                                           half_tile((w1_hi, w2_hi)[half], HPG // 2 * i + t).bitcast(F32),
                                           ALU.subtract).then_inc(w_ready, 1)

                pool.memset(taps_sb[:, 0:PAD], 0.0).then_inc(taps_zero, 1)
                pool.memset(half_power[:], -0.5).then_inc(const_ready, 1)
                pool.memset(ident[:], 0.0).then_inc(const_ready, 1)
                pool.wait_ge(const_ready, 2)
                pool.affine_select(out=ident[:], in_=ident[:], compare_op=ALU.not_equal, fill=1.0, base=0,
                                   pattern=[[-1, P]], channel_multiplier=1).then_inc(ident_ready, 1)
                pool.memset(prod[:], 0.0).then_inc(prod_zero, 1)
                pool.sem_inc(w_ready, CREDIT)
                link, n = linker(pool, pool_chain, 0)
                pool.wait_ge(stats1, 1)
                first_rstd(link, 0, GT)
                head_pairs(0, 0, True)
                head_pairs(0, 1, True)
                pool.wait_ge(stats1, 2)
                first_rstd(link, GT, NT)
                over_tiles(pool, tile)
                second_rstd(NT // GT - 1)

            @block.vector
            def _(dve):
                def first_stats(lo, hi):
                    for T in range(lo, hi):
                        if T % GT == 0:
                            dve.wait_ge(dma_x[T // GT], 16)
                        last = dve.bn_stats(st1[:, T, :], xres[:, T, :])
                    last.then_inc(st1_ready, 1)
                    dve.wait_ge(st1_ready, 1 if lo == 0 else 2)
                    for T in range(lo, hi):
                        last = dve.bn_aggr(mv1[:, T, :], st1[:, T, :])
                    last.then_inc(stats1, 1)

                def products(T, k, h, piece):
                    n_in_tile = 2 * h + piece
                    dve.wait_ge(conv_done, 4 * T + n_in_tile + 1)
                    for s, lt in enumerate(PIECES[piece]):
                        y_at = (2 * piece + s) * 512
                        q_at = (((k % 2) * LC + lt) * 2 + h) * NB * WRAP
                        p_at = piece * BUF + s * NB * SPAN
                        dve.tensor_tensor(free_view(prod, p_at, [[ROW, ND], [SPAN, NB], [1, R]]),
                                          free_view(ps_y, y_at, [[NB * R, ND], [R, NB], [1, R]]),
                                          free_view(qT, q_at, [[1, ND], [WRAP, NB], [1, R]]), ALU.mult)
                        dve.tensor_tensor(free_view(prod, p_at + (ND + 1) * ROW + 1,
                                                    [[ROW + 1, ND - 1], [SPAN, NB], [1, R]]),
                                          free_view(ps_y, y_at + NB * R, [[NB * R, ND - 1], [R, NB], [1, R]]),
                                          free_view(qT, q_at, [[0, ND - 1], [WRAP, NB], [1, R]]), ALU.mult)
                        last = dve.tensor_tensor(free_view(prod, p_at + ND * ROW, [[SPAN, NB], [R // 2, 2], [1, R // 2]]),
                                                 free_view(ps_y, y_at + ND * NB * R,
                                                           [[R // 2, NB], [0, 2], [1, R // 2]]),
                                                 free_view(qT, q_at + ND, [[WRAP, NB], [R // 2, 2], [1, R // 2]]),
                                                 ALU.mult)
                    last.then_inc(y_used, 1)

                def add_terms(parity, piece):
                    dve.tensor_reduce(free_view(summed, parity * ROW, [[1, ROW]]),
                                      free_view(prod, piece * BUF, [[1, ROW], [ROW, TERMS]]), AX_X, ALU.add
                                      ).then_inc(terms_summed, 1)

                def fold(T, k, c, h, piece):
                    dve.wait_ge(terms_summed, 3 * T + c)
                    at = (k + c) % 2 * ROW
                    lt0, lt1 = PIECES[piece]
                    m_at = ((k % 2) * LC + lt0) * P + h * NB * R
                    m_step = (lt1 - lt0) * P
                    over = SPAN - R
                    dve.tensor_tensor(free_view(mixT, m_at, [[m_step, 2], [R, NB], [1, over]]),
                                      free_view(summed, at, [[NB * SPAN, 2], [SPAN, NB], [1, over]]),
                                      free_view(summed, at + R, [[NB * SPAN, 2], [SPAN, NB], [1, over]]), ALU.add)
                    dve.tensor_copy(free_view(mixT, m_at + over, [[m_step, 2], [R, NB], [1, R - over]]),
                                    free_view(summed, at + over, [[NB * SPAN, 2], [SPAN, NB], [1, R - over]])
                                    ).then_inc(mix_ready, 1)

                def reduce_piece(T, k, c, n_in_tile):
                    if not (isinstance(T, int) and 3 * T + c <= 2):
                        dve.wait_ge(mix_ready, 3 * T + c - 2)
                    dve.wait_ge(y_used, 4 * T + n_in_tile + 3)
                    add_terms((k + c) % 2, n_in_tile % 2)

                def tile(i, k, ahead, group_done):
                    T = GT * i + k
                    if not (isinstance(T, int) and T == 0):
                        dve.wait_ge(terms_added, T)
                    products(T, k, 0, 1)
                    reduce_piece(T, k, 2, 1)
                    products(T, k, 1, 0)
                    fold(T, k, 2, 0, 1)
                    reduce_piece(T, k, 3, 2)
                    products(T, k, 1, 1)
                    fold(T, k, 3, 1, 0)
                    if ahead:
                        dve.wait_ge(qT_ready, T + 2)
                        products(T + 1, k + 1, 0, 0)
                        reduce_piece(T + 1, k + 1, 1, 0)
                    if group_done:
                        dve.wait_ge(rstd2, i)
                    dve.wait_ge(out_turned, T + 1)
                    dve.scalar_tensor_tensor(out=xtile(T), in0=ps_o[:], scalar=gate_tanh[:, 0:1], in1=xtile(T),
                                             op0=ALU.mult, op1=ALU.add).then_inc(y1_ready, 1)
                    if ahead:
                        fold(T + 1, k + 1, 1, 0, 0)
                    dve.wait_ge(y1_ready, T + 1)
                    standalone(dve)
                    dve.bn_stats(st2[:, k, :], xtile(T)).then_inc(dve_chain, 1)
                    dve.wait_ge(dve_chain, T + 1)
                    standalone(dve)
                    dve.bn_aggr(mv2[:, k, :], st2[:, k, :]).then_inc(stats2, 1)

                dve.wait_ge(dma_taps_in, 32)
                dve.wait_ge(taps_zero, 1)
                dve.tensor_tensor(taps_sb[:, PAD:PAD + 1], taps_sb[:, PAD:PAD + 1], skip_sb[:], ALU.add
                                  ).then_inc(taps_ready, 1)
                dve.sem_inc(y_used, CREDIT)
                first_stats(0, GT)
                first_stats(GT, NT)
                dve.wait_ge(prod_zero, 1)
                dve.wait_ge(qT_ready, 1)
                products(0, 0, 0, 0)
                reduce_piece(0, 0, 1, 0)
                fold(0, 0, 1, 0, 0)
                dve.wait_ge(tanh_ready, 1)
                over_tiles(dve, tile)

        with ExitStack() as scope:
            hold_weights(RESIDENT, NH, scope, "b")
            xT_hi = sb("xT_hi", [P, LC, 512], F32R, scope)
            xT_lo = sb("xT_lo", [P, LC, 512], F32R, scope)
            h_full = sb("h_full", [P, 2, 512], F32, scope)
            h_hi = sb("h_hi", [P, 2, 512], F32R, scope)
            h_lo = sb("h_lo", [P, 2, 512], F32R, scope)
            vec = sb("vec", [P, 3, D], F32, scope)
            st3 = sb("st3", [P, GT, 6], F32, scope)
            mv3 = sb("mv3", [P, GT, 2], F32, scope)
            ln3 = sb("ln3", [P, 4, GT], F32, scope)
            acc = scope.enter_context(nc.psum_tensor("acc", [P, GT, 512], F32))
            ps_h = scope.enter_context(nc.psum_tensor("ps_h", [P, 2, 512], F32))
            ps_t = scope.enter_context(nc.psum_tensor("ps_t", [P, 2, 512], F32))
            block = scope.enter_context(nc.Block())
            HALVES = 2 * NH
            EARLY = 2 * RESIDENT

            def stage_value(layer, s):
                if isinstance(layer, int) and layer == 0:
                    return 16 * ((s - EARLY) // WSLOTS + 1)
                return 16 * ((HALVES - EARLY) // WSLOTS + (HALVES // WSLOTS) * (layer - 1) + s // WSLOTS + 1)

            def weight_lo_on(eng, L, t):
                for half, hi, lo in ((0, w1_hi, w1_lo), (1, w2_hi, w2_lo)):
                    s = 2 * t + half
                    eng.wait_ge(w_hi_ready, HALVES * L + s + 1)
                    eng.tensor_tensor(lo[t], wstage[:, s % WSLOTS, :], hi[t].bitcast(F32), ALU.subtract
                                      ).then_inc(w_ready, 1)

            @block.sync
            def _(sp):
                def load_vectors(L, norm):
                    sp.dma_start(vec[:, 0, :], across(bias2, L)).then_inc(dma_vec, 16)
                    if norm:
                        sp.dma_start(vec[:, 1, :], across(gamma, L)).then_inc(dma_vec, 16)
                        sp.dma_start(vec[:, 2, :], across(beta, L)).then_inc(dma_vec, 16)

                def across(table, L):
                    row = table[bass.ds(L, 1)]
                    return bass.AP(tensor=row.tensor, offset=row.offset, ap=[[0, P], [1, D]])

                def load_half(L, s, wait):
                    if wait:
                        sp.wait_ge(w_ready, CREDIT + HALVES * L + s - WSLOTS + 1)
                    sp.dma_start(wstage[:, s % WSLOTS, :], flat(weights[bass.ds(L, 1), s // 2, s % 2])
                                 ).then_inc(dma_w[s % WSLOTS], 16)

                for s in range(EARLY, HALVES):
                    load_half(0, s, s - EARLY >= WSLOTS)
                    if s == EARLY + 2:
                        load_vectors(0, True)

                def layer(L, last_norm):
                    for s in range(HALVES):
                        load_half(L + 1, s, True)
                    sp.wait_ge(x_ready, NT * (L + 2))
                    load_vectors(L + 1, not last_norm)

                with sp.Fori(0, NL - 2) as L:
                    layer(L, False)
                layer(NL - 2, True)
                sp.wait_ge(w_ready, CREDIT + HALVES * NL)
                for g in range(NG):
                    if g:
                        sp.wait_ge(fin_ready, GT * g)
                    sp.dma_start(wstage[:, :, :], y1_dram[GT * g:GT * g + GT].rearrange("t p d -> p t d")
                                 ).then_inc(dma_base, 16)
                    sp.wait_ge(fin_ready, GT * g + GT)
                    sp.dma_start(out[GT * g:GT * g + GT].rearrange("t p d -> p t d"), xres[:, GT * g:GT * g + GT, :]
                                 ).then_inc(dma_out, 16)
                sp.wait_ge(dma_out, 16 * NG)

            @block.tensor
            def _(pe):
                def turn(n, g, c):
                    if c == 0:
                        pe.wait_ge(x_ready, GT * n + GT)
                    elif c >= 2:
                        pe.wait_ge(xT_ready, LC * n + c - 1)
                    for j in range(GT):
                        last = pe.transpose(ps_t[:, c % 2, j * P:(j + 1) * P], xres[:, GT * g + j, c * P:(c + 1) * P],
                                            ident[:])
                    last.then_inc(x_turned, 1)

                def up(L, n, g, t):
                    if g == 0:
                        pe.wait_ge(w_ready, CREDIT + HALVES * L + 2 * t + 1)
                    for c in range(LC):
                        if t == 0:
                            pe.wait_ge(xT_ready, LC * n + c + 1)
                        cs = slice(c * P, (c + 1) * P)
                        pe.matmul(ps_h[:, t % 2, :], w1_hi[t][:, cs], xT_hi[:, c, :], start=(c == 0), stop=False)
                        pe.matmul(ps_h[:, t % 2, :], w1_hi[t][:, cs], xT_lo[:, c, :], start=False, stop=False)
                        last = pe.matmul(ps_h[:, t % 2, :], w1_lo[t][:, cs], xT_hi[:, c, :], start=False,
                                         stop=(c == LC - 1))
                    last.then_inc(mm1_done, 1)

                def down(L, n, g, t, tiles):
                    if g == 0:
                        pe.wait_ge(w_ready, CREDIT + HALVES * L + 2 * t + 2)
                    pe.wait_ge(h_ready, NH * n + t + 1)
                    for j in tiles:
                        if t == 0:
                            pe.wait_ge(acc_free, GT * n + j + 1)
                        js = slice(j * P, (j + 1) * P)
                        pe.matmul(acc[:, j, :], h_hi[:, t % 2, js], w2_hi[t], start=(t == 0), stop=False)
                        pe.matmul(acc[:, j, :], h_hi[:, t % 2, js], w2_lo[t], start=False, stop=False)
                        last = pe.matmul(acc[:, j, :], h_lo[:, t % 2, js], w2_hi[t], start=False, stop=(t == NH - 1))
                        if t == NH - 1:
                            last.then_inc(mm2_done, 1)
                    if t < NH - 1:
                        last.then_inc(mm2_done, 1)

                def group(L, g, more):
                    n = NG * L + g
                    for t in range(NH):
                        up(L, n, g, t)
                        if t:
                            down(L, n, g, t - 1, range(GT))
                    if more:
                        g2 = (g + 1) % NG
                        turn(n + 1, g2, 0)
                        turn(n + 1, g2, 1)
                        down(L, n, g, NH - 1, [0, 1])
                        turn(n + 1, g2, 2)
                        down(L, n, g, NH - 1, [2])
                        turn(n + 1, g2, 3)
                        down(L, n, g, NH - 1, [3])
                    else:
                        down(L, n, g, NH - 1, range(GT))

                for c in range(LC):
                    turn(0, 0, c)
                with pe.Fori(0, NL - 1) as L:
                    for g in range(NG):
                        group(L, g, True)
                for g in range(NG):
                    group(NL - 1, g, g < NG - 1)

            @block.scalar
            def _(act):
                def weight_hi(L, t):
                    for half, table in ((0, w1_hi), (1, w2_hi)):
                        s = 2 * t + half
                        act.wait_ge(dma_w[s % WSLOTS], stage_value(L, s))
                        act.activation(table[t], wstage[:, s % WSLOTS, :], ACT.Copy).then_inc(w_hi_ready, 1)

                def input_hi(n, c):
                    act.wait_ge(x_turned, LC * n + c + 1)
                    act.activation(xT_hi[:, c, :], ps_t[:, c % 2, :], ACT.Copy).then_inc(xT_hi_ready, 1)

                def gelu(L, n, t):
                    act.wait_ge(mm1_done, NH * n + t + 1)
                    bias = b1[:, bass.ds(NH * L + t, 1)]
                    standalone(act)
                    act.activation(h_hi[:, t % 2, :], ps_h[:, t % 2, :], ACT.Gelu, bias=bias)
                    act.activation(h_full[:, t % 2, :], ps_h[:, t % 2, :], ACT.Gelu, bias=bias).then_inc(gelu_done, 1)

                def group(L, g, more, reload):
                    n = NG * L + g
                    for t in range(1, NH):
                        gelu(L, n, t)
                        if reload and t >= 2:
                            weight_hi(L + 1, t - 2)
                    if more:
                        input_hi(n + 1, 0)
                        input_hi(n + 1, 1)
                    if reload:
                        act.wait_ge(mm2_done, MM2 * n + NH - 1)
                        weight_hi(L + 1, NH - 2)
                    if more:
                        input_hi(n + 1, 2)
                        input_hi(n + 1, 3)
                    if reload:
                        act.wait_ge(mm2_done, MM2 * n + MM2)
                        weight_hi(L + 1, NH - 1)
                    if more:
                        gelu(L + (g + 1) // NG, n + 1, 0)

                for c in range(LC):
                    input_hi(0, c)
                for t in range(RESIDENT, NH):
                    if t == RESIDENT + 2:
                        gelu(0, 0, 0)
                    weight_hi(0, t)
                with act.Fori(0, NL - 1) as L:
                    for g in range(NG):
                        group(L, g, True, g == NG - 1)
                for g in range(NG):
                    group(NL - 1, g, g < NG - 1, False)

            @block.vector
            def _(dve):
                def weight_lo(L, t):
                    weight_lo_on(dve, L, t)

                def input_lo(n, c):
                    dve.wait_ge(xT_hi_ready, LC * n + c + 1)
                    dve.tensor_tensor(xT_lo[:, c, :], ps_t[:, c % 2, :], xT_hi[:, c, :].bitcast(F32), ALU.subtract
                                      ).then_inc(xT_ready, 1)

                def read_out(n, g, j):
                    dve.wait_ge(mm2_done, MM2 * n + NH - 1 + j + 1)
                    dve.wait_ge(biased, GT * n + j + 1)
                    dve.tensor_tensor(xres[:, GT * g + j, :], acc[:, j, :], xres[:, GT * g + j, :], ALU.add
                                      ).then_inc(acc_free, 1)

                def tile_stats(n, g, j):
                    dve.wait_ge(acc_free, GT * (n + 1) + j + 1)
                    dve.bn_stats(st3[:, j, :], xres[:, GT * g + j, :]).then_inc(sumsq, 1)

                def finish(n, g, j):
                    dve.wait_ge(acc_free, GT * (n + 1) + j + 1)
                    if j == 0:
                        dve.wait_ge(dma_base, 16 * (g + 1))
                    dve.scalar_tensor_tensor(out=xres[:, GT * g + j, :], in0=xres[:, GT * g + j, :],
                                             scalar=gate_tanh[:, 1:2], in1=wstage[:, j, :], op0=ALU.mult,
                                             op1=ALU.add).then_inc(fin_ready, 1)

                def hidden_lo(n, t):
                    dve.wait_ge(gelu_done, NH * n + t + 1)
                    dve.tensor_tensor(h_lo[:, t % 2, :], h_full[:, t % 2, :], h_hi[:, t % 2, :].bitcast(F32),
                                      ALU.subtract).then_inc(h_ready, 1)

                def group(L, g, more, reload, norm):
                    n = NG * L + g
                    for t in range(1, NH):
                        hidden_lo(n, t)
                        if reload and t >= 2:
                            weight_lo(L + 1, t - 2)
                    close = tile_stats if norm else finish
                    steps = [(input_lo, 0), (input_lo, 1), (read_out, 0), (input_lo, 2), (read_out, 1), (close, 0),
                             (input_lo, 3), (read_out, 2), (close, 1), (read_out, 3), (hidden_lo, 0), (close, 2),
                             (close, 3)]
                    for step, a in steps:
                        if step is input_lo or step is hidden_lo:
                            if more:
                                step(n + 1, a)
                        else:
                            step(n, g, a)
                    if norm:
                        dve.wait_ge(sumsq, GT * n + GT)
                        standalone(dve)
                        for j in range(GT):
                            last = dve.bn_aggr(mv3[:, j, :], st3[:, j, :])
                        last.then_inc(stats3, 1)
                dve.sem_inc(acc_free, GT)
                for c in range(LC):
                    input_lo(0, c)
                for t in range(RESIDENT, NH):
                    if t == RESIDENT + 2:
                        hidden_lo(0, 0)
                    weight_lo(0, t)
                with dve.Fori(0, NL - 1) as L:
                    for g in range(NG):
                        group(L, g, True, g == NG - 1, True)
                for g in range(NG):
                    group(NL - 1, g, g < NG - 1, False, False)

            @block.gpsimd
            def _(pool):
                base = 2 * CH + NG * CH
                per = CH + 2

                def group(L, g, norm):
                    n = NG * L + g
                    pool.wait_ge(x_turned, LC * n + LC)
                    if norm:
                        pool.wait_ge(dma_vec, 48 * L + 48)
                    else:
                        pool.wait_ge(dma_vec, 48 * L + 16)
                    for j in range(GT):
                        xj = xres[:, GT * g + j, :]
                        pool.tensor_tensor(xj, xj, vec[:, 0, :], ALU.add).then_inc(biased, 1)
                    if not norm:
                        return
                    if g == NG - 1:
                        pool.wait_ge(w_ready, CREDIT + HALVES * (L + 1) + 2 * NH - 4)
                        weight_lo_on(pool, L + 1, NH - 2)
                        weight_lo_on(pool, L + 1, NH - 1)
                    link, k = linker(pool, pool_chain, base + per * n)
                    pool.wait_ge(stats3, n + 1)
                    rs, nm = ln3[:, 2, :], ln3[:, 3, :]
                    ln_done = rstd_chain(pool, link, mv3[:, :, 0], mv3[:, :, 1], ln3[:, 0, :], ln3[:, 1, :], rs, nm)
                    link(ln_done)
                    standalone(pool)
                    for j in range(GT):
                        xj = xres[:, GT * g + j, :]
                        last = pool.tensor_scalar(xj, xj, rs[:, j:j + 1], nm[:, j:j + 1], ALU.mult, ALU.add)
                    link(last)
                    for j in range(GT):
                        xj = xres[:, GT * g + j, :]
                        last = pool.tensor_tensor(xj, xj, vec[:, 1, :], ALU.mult)
                    last.then_inc(scaled, 1)
                    pool.wait_ge(scaled, n + 1)
                    for j in range(GT):
                        xj = xres[:, GT * g + j, :]
                        pool.tensor_tensor(xj, xj, vec[:, 2, :], ALU.add).then_inc(x_ready, 1)
                    assert k[0] == per

                with pool.Fori(0, NL - 1) as L:
                    for g in range(NG):
                        group(L, g, True)
                for g in range(NG):
                    group(NL - 1, g, False)


def kernel(**inputs):
    import numpy as _np
    import concourse.bacc as _bacc
    from concourse import mybir as _mybir
    from concourse.bass_utils import run_bass_kernel_spmd as _run

    a = {k: _np.asarray(v) for k, v in inputs.items()}
    x, c = a["x"], a["ctx_2048"]
    B, S, D = x.shape
    R, NT = 8, B * S // 128

    def tiles(m):
        return m.reshape(B, NT, 2, R, D).transpose(1, 2, 0, 3, 4).reshape(NT, 128, D)

    w1, w2 = a["L0_ffn_W1"], a["L0_ffn_W2"]
    NL, H, _ = w1.shape
    LC, NH = D // 128, H // 128
    w1t = w1.reshape(NL, NH, 128, LC, 128).transpose(0, 1, 4, 3, 2).reshape(NL, NH, 1, 128, D)
    w2t = w2.reshape(NL, D, NH, 128).transpose(0, 2, 3, 1).reshape(NL, NH, 1, 128, D)
    arrays = {
        "x": tiles(x),
        "ctx_in": tiles(c.reshape(B, S, LC, 128)[..., ::-1].reshape(B, S, D)),
        "gates": _np.concatenate([a["g_xattn"], a["g_ffn"]]),
        "taps": a["L0_xattn_ssm_kernel"],
        "skip": a["L0_xattn_D"].reshape(-1, 1),
        "weights": _np.concatenate([w1t, w2t], axis=2),
        "bias1": a["L0_ffn_B1"].reshape(NL, NH, 128).transpose(2, 0, 1).reshape(128, NL * NH),
        "bias2": a["L0_ffn_B2"],
        "gamma": a["L0_ffn_LN_G"],
        "beta": a["L0_ffn_LN_B"],
    }
    arrays = {k: _np.ascontiguousarray(v) for k, v in arrays.items()}
    nc = _bacc.Bacc("TRN2", target_bir_lowering=False, num_devices=1)
    args = [nc.dram_tensor(k, v.shape, _mybir.dt.float32, kind="ExternalInput").ap() for k, v in arrays.items()]
    args.append(nc.dram_tensor("mixed_out", (NT, 128, D), _mybir.dt.float32, kind="ExternalOutput").ap())
    mixer_mlp_kernel(nc, *args)
    r = _run(nc, [arrays], core_ids=[0])
    y = r.results[0]["mixed_out"]
    return y.reshape(NT, 2, B, R, D).transpose(2, 0, 1, 3, 4).reshape(B, S, D)
```

```python
from contextlib import ExitStack

import concourse.bass as bass
from concourse import mybir

P = 128
F32 = mybir.dt.float32
F32R = mybir.dt.float32r
ALU = mybir.AluOpType
ACT = mybir.ActivationFunctionType
AX_X = mybir.AxisListType.X


def free_view(tensor, offset, dims):
    whole = tensor[:]
    return bass.AP(tensor=whole.tensor, offset=whole.offset + offset, ap=[list(whole.ap[0])] + dims)


def flat(ap):
    return ap.rearrange("a p n -> p (a n)")


def flat_free(ap):
    return ap.rearrange("p a n -> p (a n)")


def mixer_mlp_kernel(nc, x, ctx_in, gates, taps, skip, weights, bias1, bias2, gamma, beta, out):
    NT, _, D = x.shape
    NL, NH = weights.shape[0], weights.shape[1]
    HEADS = taps.shape[0]
    LC = D // P
    NB, R = 8, 8
    ND = 4
    PAIRS = ND * NB * R + NB * R // 2
    WRAP = R + ND
    TERMS, SPAN = 2 * ND, R + ND - 1
    NG, GT = 4, NT // 4
    EPS = 1e-5
    PAD = P
    RESIDENT = 3 * NH // 4
    PIECES = ((0, 3), (1, 2))
    WSLOTS = 4
    CREDIT = MIXSLOTS = 3
    Y_CREDIT = 2
    HALVES = 2 * NH
    EARLY = 2 * RESIDENT
    X_LOADS = ((0, 2), (2, 4), (4, 8), (8, 12), (12, 16))
    X_STATS = ((0, 2), (2, 8), (8, 12), (12, 16))

    y1_dram = nc.dram_tensor("mixed_scratch", (NT, P, D), F32, kind="Internal").ap()
    taps_dram = nc.dram_tensor("padded_taps_scratch", (HEADS, PAD + D), F32, kind="Internal").ap()

    with ExitStack() as ctx:
        def sb(name, shape, dt=F32, scope=ctx):
            return scope.enter_context(nc.sbuf_tensor(name, shape, dt))

        def sem(name):
            return ctx.enter_context(nc.semaphore(name))

        w1_hi, w1_lo, w2_hi, w2_lo = ([None] * NH for _ in range(4))
        held = {}

        def hold_weights(lo, hi, scope, tag):
            for name, table in (("w1_hi", w1_hi), ("w1_lo", w1_lo), ("w2_hi", w2_hi), ("w2_lo", w2_lo)):
                part = sb(f"{name}_{tag}", [P, hi - lo, D], F32R, scope)
                held.setdefault(id(table), part)
                for t in range(lo, hi):
                    table[t] = part[:, t - lo, :]

        def half_tile(table, t):
            return flat_free(held[id(table)][:, bass.ds(t, 1), :])

        hold_weights(0, RESIDENT, ctx, "a")
        xres = sb("xres", [P, NT, D])
        wstage = sb("wstage", [P, WSLOTS, D])
        ident = sb("ident", [P, P])
        b1 = sb("b1", [P, NL * NH])
        gate = sb("gate", [P, 2])
        gate_tanh = sb("gate_tanh", [P, 2])
        table_first = sb("table_first", [P, 1])
        half_power = sb("half_power", [P, NT])
        st2 = sb("st2", [P, GT, 6])
        mv2 = sb("mv2", [P, GT, 2])
        ln2 = sb("ln2", [P, 4, GT])

        dma_const = sem("dma_const")
        dma_taps_in = sem("dma_taps_in")
        dma_taps_out = sem("dma_taps_out")
        dma_x = [sem(f"dma_x{i}") for i in range(len(X_LOADS))]
        dma_c = [sem(f"dma_c{i}") for i in range(2)]
        dma_g = [sem(f"dma_g{i}") for i in range(2)]
        dma_wa = [sem(f"dma_wa{i}") for i in range(MIXSLOTS)]
        dma_w = [sem(f"dma_w{i}") for i in range(WSLOTS)]
        dma_y1 = [sem(f"dma_y1_{i}") for i in range(GT)]
        dma_vec = sem("dma_vec")
        dma_base = sem("dma_base")
        dma_out = sem("dma_out")
        ident_ready = sem("ident_ready")
        const_ready = sem("const_ready")
        wait_taken = sem("wait_taken")
        tanh_ready = sem("tanh_ready")
        taps_zero = sem("taps_zero")
        prod_zero = sem("prod_zero")
        taps_ready = sem("taps_ready")
        dve_chain = sem("dve_chain")
        pool_chain = sem("pool_chain")
        stats1 = sem("stats1")
        st1_ready = sem("st1_ready")
        terms_added = sem("terms_added")
        terms_summed = sem("terms_summed")
        mix_copied = sem("mix_copied")
        rstd1 = sem("rstd1")
        qn_ready = sem("qn_ready")
        c_turned = sem("c_turned")
        q_turned = sem("q_turned")
        qT_ready = sem("qT_ready")
        cT_ready = sem("cT_ready")
        pairs_ready = sem("pairs_ready")
        conv_done = sem("conv_done")
        y_used = sem("y_used")
        mix_ready = sem("mix_ready")
        out_turned = sem("out_turned")
        y1_ready = sem("y1_ready")
        stats2 = sem("stats2")
        rstd2 = sem("rstd2")
        x_ready = sem("x_ready")
        w_hi_ready = sem("w_hi_ready")
        w_ready = sem("w_ready")
        x_turned = sem("x_turned")
        xT_hi_ready = sem("xT_hi_ready")
        xT_ready = sem("xT_ready")
        mm1_done = sem("mm1_done")
        gelu_done = sem("gelu_done")
        h_ready = sem("h_ready")
        mm2_done = sem("mm2_done")
        biased = sem("biased")
        acc_free = sem("acc_free")
        st3_ready = sem("st3_ready")
        stats3 = sem("stats3")
        scaled = sem("scaled")
        fin_ready = sem("fin_ready")

        def standalone(eng):
            eng.sem_inc(wait_taken, 1)

        MM2 = NH - 1 + GT

        def rstd_chain(pool, link, mean, var, ve, tmp, rstd, nmr):
            standalone(pool)
            link(pool.tensor_scalar(ve, var, EPS, None, ALU.add))
            link(pool.tensor_tensor(rstd, ve, half_power[:, 0:ve.shape[-1]], ALU.pow))
            link(pool.tensor_tensor(tmp, rstd, rstd, ALU.mult))
            link(pool.tensor_tensor(tmp, tmp, ve, ALU.mult))
            standalone(pool)
            link(pool.tensor_scalar(tmp, tmp, -0.5, 1.5, ALU.mult, ALU.add))
            link(pool.tensor_tensor(rstd, rstd, tmp, ALU.mult))
            link(pool.tensor_tensor(tmp, mean, rstd, ALU.mult))
            standalone(pool)
            return pool.tensor_scalar(nmr, tmp, -1.0, None, ALU.mult)

        CH = 7

        def linker(eng, chain, base):
            n = [0]

            def link(ins):
                n[0] += 1
                ins.then_inc(chain, 1)
                eng.wait_ge(chain, base + n[0])
            return link, n

        def xtile(T):
            return flat_free(xres[:, bass.ds(T, 1), :])

        def store_y1(sp, T, k):
            sp.wait_ge(y1_ready, T + 1)
            sp.dma_start(flat(y1_dram[bass.ds(T, 1)]), xtile(T)).then_inc(dma_y1[k], 16)

        def load_half(sp, L, s, wait):
            if wait:
                sp.wait_ge(w_ready, CREDIT + HALVES * L + s - WSLOTS + 1)
            sp.dma_start(wstage[:, s % WSLOTS, :], flat(weights[bass.ds(L, 1), s // 2, s % 2])
                         ).then_inc(dma_w[s % WSLOTS], 16)

        def row_stats(dve, T, k):
            dve.wait_ge(y1_ready, T + 1)
            standalone(dve)
            dve.bn_stats(st2[:, k, :], xtile(T)).then_inc(dve_chain, 1)

        def combine_stats(dve, T, k):
            dve.wait_ge(dve_chain, T + 1)
            standalone(dve)
            dve.bn_aggr(mv2[:, k, :], st2[:, k, :]).then_inc(stats2, 1)

        def second_rstd(pool, i):
            link, n = linker(pool, pool_chain, len(X_STATS) * CH + CH * i)
            pool.wait_ge(stats2, GT * i + GT)
            rstd_chain(pool, link, mv2[:, :, 0], mv2[:, :, 1], *[ln2[:, r, :] for r in range(4)]).then_inc(rstd2, 1)
            assert n[0] == CH

        with ExitStack() as scope:
            taps_sb = sb("taps_sb", [HEADS, PAD + D], F32, scope)
            skip_sb = sb("skip_sb", [HEADS, 1], F32, scope)
            ca = sb("ca", [P, 2, D], F32, scope)
            qn = sb("qn", [P, 2, D], F32, scope)
            qT = sb("qT", [P, 2, LC, 2, NB, WRAP], F32, scope)
            cT = sb("cT", [P, LC, 2, NB, WRAP], F32, scope)
            pairs = sb("pairs", [P, 2, LC, PAIRS], F32, scope)
            lags = sb("lags", [P, 2, D], F32, scope)
            prod = sb("prod", [P, 2, TERMS, 2, NB, SPAN], F32, scope)
            summed = sb("summed", [P, 2, 2, NB, SPAN], F32, scope)
            mixT = sb("mixT", [P, 2, LC, P], F32, scope)
            st1 = sb("st1", [P, NT, 6], F32, scope)
            mv1 = sb("mv1", [P, NT, 2], F32, scope)
            ln1 = sb("ln1", [P, 4, NT], F32, scope)
            ps_y = scope.enter_context(nc.psum_tensor("ps_y", [P, 4, 512], F32))
            ps_q = scope.enter_context(nc.psum_tensor("ps_q", [P, LC, P], F32))
            ps_c = scope.enter_context(nc.psum_tensor("ps_c", [P, LC, P], F32))
            ps_o = scope.enter_context(nc.psum_tensor("ps_o", [P, LC * P], F32))
            ps_s = scope.enter_context(nc.psum_tensor("ps_s", [P, 512], F32))

            ROW = 2 * NB * SPAN
            BUF = TERMS * ROW

            def toeplitz(head):
                first = taps_dram[bass.ds(head, 1), 1:1 + P]
                return bass.AP(tensor=first.tensor, offset=first.offset, ap=[[1, P], [1, D]])

            HPG = 2 * RESIDENT * GT // NT

            def halves(i, k):
                for m in range(HPG * k // GT, HPG * (k + 1) // GT):
                    yield (m % MIXSLOTS, HPG * i + m, HPG // MIXSLOTS * i + m // MIXSLOTS + 1,
                           HPG // 2 * i + m // 2, m % 2)

            def is_tile(T, number):
                return isinstance(T, int) and T == number

            def last_two(T):
                return isinstance(T, int) and T >= NT - 2

            def over_tiles(eng, tile):
                tile(0, 0, True, False)
                with eng.Fori(0, NT // GT - 1) as i:
                    for k in range(1, GT):
                        tile(i, k, True, False)
                    tile(i + 1, 0, True, True)
                for k in range(1, GT):
                    tile(NT // GT - 1, k, k < GT - 1, False)

            block = scope.enter_context(nc.Block())

            @block.sync
            def _(sp):
                def load_x(load):
                    lo, hi = X_LOADS[load]
                    sp.dma_start(xres[:, lo:hi, :], x[lo:hi].rearrange("t p d -> p t d")).then_inc(dma_x[load], 16)

                sp.dma_start(taps_sb[:, PAD:], taps).then_inc(dma_taps_in, 16)
                sp.dma_start(skip_sb[:], skip).then_inc(dma_taps_in, 16)
                sp.dma_start(ca[:, 0, :], ctx_in[0]).then_inc(dma_c[0], 16)
                load_x(0)
                sp.wait_ge(taps_ready, 1)
                sp.dma_start(taps_dram, taps_sb[:]).then_inc(dma_taps_out, 16)
                load_x(1)
                sp.wait_ge(dma_taps_out, 16)
                for h in range(2):
                    sp.dma_start(lags[:, h, :], toeplitz(h)).then_inc(dma_g[h], 16)
                load_x(2)
                sp.dma_start(ca[:, 1, :], ctx_in[1]).then_inc(dma_c[1], 16)
                sp.dma_start(gate[:], bass.AP(tensor=gates.tensor, offset=0, ap=[[0, P], [1, 2]])
                             ).then_inc(dma_const, 16)
                sp.dma_start(b1[:], bias1).then_inc(dma_const, 16)
                load_x(3)
                load_x(4)

                def load_halves(i, k):
                    for slot, m, _, t, half in halves(i, k):
                        sp.wait_ge(w_ready, m + 1)
                        sp.dma_start(wstage[:, slot, :], flat(weights[0, bass.ds(t, 1), half])
                                     ).then_inc(dma_wa[slot], 16)

                def tile(i, k, ahead, _):
                    T = GT * i + k
                    if not last_two(T):
                        sp.wait_ge(c_turned, T + 1)
                        sp.dma_start(ca[:, k % 2, :], flat(ctx_in[bass.ds(T + 2, 1)])).then_inc(dma_c[k % 2], 16)
                    if is_tile(T, NT - 1):
                        load_halves(i, k)
                    for h in range(2):
                        if ahead:
                            sp.wait_ge(conv_done, 4 * T + 2 * h + 2)
                            sp.dma_start(lags[:, h, :], toeplitz(2 * T + 2 + h)).then_inc(dma_g[h], 16)
                        if h == 0 and not is_tile(T, 0):
                            store_y1(sp, T - 1, (k - 1) % GT)
                    if not is_tile(T, NT - 1):
                        load_halves(i, k)

                over_tiles(sp, tile)
                sp.wait_ge(w_ready, CREDIT + EARLY)
                for s in range(EARLY, EARLY + WSLOTS):
                    load_half(sp, 0, s, False)

            @block.tensor
            def _(pe):
                def turn_context(i, k, T, first=False):
                    if not first:
                        pe.wait_ge(cT_ready, T)
                    pe.wait_ge(dma_c[k % 2], 32 * i + 16 * (k // 2) + 16)
                    for c in range(LC):
                        last = pe.transpose(ps_c[:, c, :], ca[:, k % 2, c * P:(c + 1) * P], ident[:])
                    last.then_inc(c_turned, 1)

                def turn_q(k, T, first=False):
                    if not first:
                        pe.wait_ge(qT_ready, T)
                    pe.wait_ge(qn_ready, T + 1)
                    for c in range(LC):
                        last = pe.transpose(ps_q[:, c, :], qn[:, k % 2, c * P:(c + 1) * P], ident[:])
                    last.then_inc(q_turned, 1)

                def conv(T, h, piece):
                    if piece == 0:
                        pe.wait_ge(pairs_ready, 2 * T + h + 1)
                        pe.wait_ge(dma_g[h], 16 * T + 16)
                    pe.wait_ge(y_used, 4 * T + 2 * h + piece + 1)
                    for s, lt in enumerate(PIECES[piece]):
                        for mt in range(lt + 1):
                            last = pe.matmul(ps_y[:, 2 * piece + s, 0:PAIRS],
                                             lags[:, h, (lt - mt) * P:(lt - mt + 1) * P], pairs[:, h, mt, :],
                                             start=(mt == 0), stop=(mt == lt))
                    last.then_inc(conv_done, 1)

                def add_terms(T, n_in_tile):
                    pe.wait_ge(y_used, 4 * T + n_in_tile + 3)
                    buf = (n_in_tile % 2) * BUF
                    for a in range(TERMS):
                        pe.matmul(ps_s[:, 0:2 * NB * R], ident[:], free_view(prod, buf + a * ROW, [[SPAN, 2 * NB], [1, R]]),
                                  start=(a == 0), stop=False, skip_group_check=True)
                    for d in range(1, ND):
                        last = pe.matmul(free_view(ps_s, 0, [[R, 2 * NB], [1, d]]), ident[:],
                                         free_view(prod, buf + (ND + d) * ROW + R, [[SPAN, 2 * NB], [1, d]]),
                                         start=False, stop=(d == ND - 1), skip_group_check=True)
                    last.then_inc(terms_added, 1)

                def turn_out(T, k):
                    pe.wait_ge(mix_ready, 3 * T + 3)
                    pe.wait_ge(mix_copied, T + 1)
                    for c in range(LC):
                        last = pe.transpose(ps_o[:, c * P:(c + 1) * P], mixT[:, k % 2, c, :], ident[:])
                    last.then_inc(out_turned, 1)

                def tile(i, k, ahead, _):
                    T = GT * i + k
                    conv(T, 0, 1)
                    if is_tile(T, 0):
                        turn_context(0, 1, 1)
                        turn_q(1, 1)
                    else:
                        turn_out(T - 1, k - 1)
                    conv(T, 1, 0)
                    if not last_two(T):
                        turn_context(i + (k + 2) // GT, (k + 2) % GT, T + 2)
                        turn_q(k + 2, T + 2)
                    conv(T, 1, 1)
                    if ahead:
                        conv(T + 1, 0, 0)
                    add_terms(T, 3)

                pe.wait_ge(ident_ready, 1)
                turn_context(0, 0, 0, first=True)
                conv(0, 0, 0)
                turn_q(0, 0, first=True)
                over_tiles(pe, tile)
                turn_out(NT - 1, GT - 1)

            @block.scalar
            def _(act):
                def normalise(T, k):
                    standalone(act)
                    act.activation(qn[:, k % 2, :], xtile(T), ACT.Identity, bias=ln1[:, 3, bass.ds(T, 1)],
                                   scale=ln1[:, 2, bass.ds(T, 1)]).then_inc(qn_ready, 1)

                def spread(source, into, base):
                    for lo, n in ((0, R), (R, ND)):
                        last = act.activation(free_view(into, base + lo, [[WRAP, LC * 2 * NB], [1, n]]),
                                              free_view(source, 0, [[R, LC * 2 * NB], [1, n]]), ACT.Copy)
                    return last

                def spread_context(T, first):
                    act.wait_ge(c_turned, T + 1)
                    if not first:
                        act.wait_ge(pairs_ready, 2 * T)
                    spread(ps_c, cT, 0).then_inc(cT_ready, 1)

                def spread_q(T, k):
                    act.wait_ge(q_turned, T + 1)
                    spread(ps_q, qT, (k % 2) * LC * 2 * NB * WRAP).then_inc(qT_ready, 1)

                def second_norm(i):
                    act.wait_ge(rstd2, i + 1)
                    for k in range(GT):
                        act.wait_ge(dma_y1[k], 16 * i + 16)
                        standalone(act)
                        act.activation(xtile(GT * i + k), xtile(GT * i + k), ACT.Identity, bias=ln2[:, 3, k:k + 1],
                                       scale=ln2[:, 2, k:k + 1]).then_inc(x_ready, 1)

                def weight_halves_hi(i, k):
                    for slot, _, use, t, half in halves(i, k):
                        act.wait_ge(dma_wa[slot], 16 * use)
                        standalone(act)
                        act.activation(half_tile((w1_hi, w2_hi)[half], t), wstage[:, slot, :], ACT.Copy
                                       ).then_inc(w_hi_ready, 1)

                def tile(i, k, ahead, group_done):
                    T = GT * i + k
                    if is_tile(T, NT - 1):
                        weight_halves_hi(i, k)
                    act.wait_ge(terms_added, T + 1)
                    m_at = ((k % 2) * LC + PIECES[1][0]) * P + NB * R
                    m_step = (PIECES[1][1] - PIECES[1][0]) * P
                    act.activation(free_view(mixT, m_at, [[m_step, 2], [1, NB * R]]),
                                   free_view(ps_s, 0, [[NB * R, 2], [1, NB * R]]), ACT.Copy).then_inc(mix_copied, 1)
                    if not last_two(T):
                        spread_context(T + 2, False)
                        spread_q(T + 2, k + 2)
                        if not is_tile(T, NT - 3):
                            normalise(T + 3, k + 3)
                    if not is_tile(T, NT - 1):
                        weight_halves_hi(i, k)
                    if group_done:
                        second_norm(i - 1)
                    if is_tile(T, 0):
                        act.wait_ge(rstd1, len(X_STATS))

                spread_context(0, True)
                act.wait_ge(rstd1, 1)
                normalise(0, 0)
                normalise(1, 1)
                spread_q(0, 0)
                act.wait_ge(dma_const, 32)
                act.activation(gate_tanh[:], gate[:], ACT.Tanh).then_inc(tanh_ready, 1)
                spread_context(1, False)
                act.wait_ge(rstd1, 2)
                normalise(2, 2)
                spread_q(1, 1)
                over_tiles(act, tile)

            @block.gpsimd
            def _(pool):
                def head_pairs(T, h, first):
                    pool.wait_ge(cT_ready, T + 1)
                    if not first:
                        pool.wait_ge(conv_done, 4 * T - 2 + 2 * h)
                    for lt in range(LC):
                        at = (lt * 2 + h) * NB * WRAP
                        pool.tensor_tensor(free_view(pairs, (h * LC + lt) * PAIRS, [[NB * R, ND], [R, NB], [1, R]]),
                                           free_view(cT, at, [[0, ND], [WRAP, NB], [1, R]]),
                                           free_view(cT, at, [[1, ND], [WRAP, NB], [1, R]]), ALU.mult)
                    at = h * NB * WRAP
                    pool.tensor_tensor(free_view(pairs, h * LC * PAIRS + ND * NB * R,
                                                 [[PAIRS, LC], [R // 2, NB], [1, R // 2]]),
                                       free_view(cT, at, [[2 * NB * WRAP, LC], [WRAP, NB], [1, R // 2]]),
                                       free_view(cT, at + ND, [[2 * NB * WRAP, LC], [WRAP, NB], [1, R // 2]]),
                                       ALU.mult).then_inc(pairs_ready, 1)

                def first_rstd(link, part):
                    pool.wait_ge(stats1, part + 1)
                    lo, hi = X_STATS[part]
                    rstd_chain(pool, link, mv1[:, lo:hi, 0], mv1[:, lo:hi, 1],
                               *[ln1[:, r, lo:hi] for r in range(4)]).then_inc(rstd1, 1)

                def weight_halves_lo(i, k):
                    for slot, m, _, t, half in halves(i, k):
                        pool.wait_ge(w_hi_ready, m + 1)
                        pool.tensor_tensor(half_tile((w1_lo, w2_lo)[half], t), wstage[:, slot, :],
                                           half_tile((w1_hi, w2_hi)[half], t).bitcast(F32), ALU.subtract
                                           ).then_inc(w_ready, 1)

                def tile(i, k, ahead, group_done):
                    T = GT * i + k
                    if ahead:
                        head_pairs(T + 1, 0, False)
                    if not is_tile(T, 0):
                        weight_halves_lo(i if k else i - 1, (k - 1) % GT)
                    if group_done:
                        second_rstd(pool, i - 1)
                    if ahead:
                        head_pairs(T + 1, 1, False)
                    if is_tile(T, 0):
                        first_rstd(link, 2)
                        first_rstd(link, 3)

                pool.memset(taps_sb[:, 0:PAD], 0.0).then_inc(taps_zero, 1)
                pool.memset(half_power[:], -0.5).then_inc(const_ready, 1)
                pool.memset(ident[:], 0.0).then_inc(const_ready, 1)
                pool.wait_ge(const_ready, 2)
                pool.affine_select(out=ident[:], in_=ident[:], compare_op=ALU.not_equal, fill=1.0, base=0,
                                   pattern=[[-1, P]], channel_multiplier=1).then_inc(ident_ready, 1)
                pool.memset(prod[:], 0.0).then_inc(prod_zero, 1)
                pool.sem_inc(w_ready, CREDIT)
                link, n = linker(pool, pool_chain, 0)
                head_pairs(0, 0, True)
                first_rstd(link, 0)
                head_pairs(0, 1, True)
                first_rstd(link, 1)
                over_tiles(pool, tile)
                weight_halves_lo(NT // GT - 1, GT - 1)

            @block.vector
            def _(dve):
                def first_stats(part):
                    lo, hi = X_STATS[part]
                    for T in range(lo, hi):
                        for load, (first, _) in enumerate(X_LOADS):
                            if T == first:
                                dve.wait_ge(dma_x[load], 16)
                        last = dve.bn_stats(st1[:, T, :], xres[:, T, :])
                    last.then_inc(st1_ready, 1)
                    dve.wait_ge(st1_ready, part + 1)
                    for T in range(lo, hi):
                        last = dve.bn_aggr(mv1[:, T, :], st1[:, T, :])
                    last.then_inc(stats1, 1)

                def products(T, k, h, piece):
                    n_in_tile = 2 * h + piece
                    dve.wait_ge(conv_done, 4 * T + n_in_tile + 1)
                    for s, lt in enumerate(PIECES[piece]):
                        y_at = (2 * piece + s) * 512
                        q_at = (((k % 2) * LC + lt) * 2 + h) * NB * WRAP
                        p_at = piece * BUF + s * NB * SPAN
                        dve.tensor_tensor(free_view(prod, p_at, [[ROW, ND], [SPAN, NB], [1, R]]),
                                          free_view(ps_y, y_at, [[NB * R, ND], [R, NB], [1, R]]),
                                          free_view(qT, q_at, [[1, ND], [WRAP, NB], [1, R]]), ALU.mult)
                        dve.tensor_tensor(free_view(prod, p_at + (ND + 1) * ROW + 1,
                                                    [[ROW + 1, ND - 1], [SPAN, NB], [1, R]]),
                                          free_view(ps_y, y_at + NB * R, [[NB * R, ND - 1], [R, NB], [1, R]]),
                                          free_view(qT, q_at, [[0, ND - 1], [WRAP, NB], [1, R]]), ALU.mult)
                        last = dve.tensor_tensor(free_view(prod, p_at + ND * ROW, [[SPAN, NB], [R // 2, 2], [1, R // 2]]),
                                                 free_view(ps_y, y_at + ND * NB * R,
                                                           [[R // 2, NB], [0, 2], [1, R // 2]]),
                                                 free_view(qT, q_at + ND, [[WRAP, NB], [R // 2, 2], [1, R // 2]]),
                                                 ALU.mult)
                    last.then_inc(y_used, 1)

                def add_terms(parity, piece):
                    dve.tensor_reduce(free_view(summed, parity * ROW, [[1, ROW]]),
                                      free_view(prod, piece * BUF, [[1, ROW], [ROW, TERMS]]), AX_X, ALU.add
                                      ).then_inc(terms_summed, 1)

                def fold(T, k, c, h, piece):
                    dve.wait_ge(terms_summed, 3 * T + c)
                    at = (k + c) % 2 * ROW
                    lt0, lt1 = PIECES[piece]
                    m_at = ((k % 2) * LC + lt0) * P + h * NB * R
                    m_step = (lt1 - lt0) * P
                    over = SPAN - R
                    dve.tensor_tensor(free_view(mixT, m_at, [[m_step, 2], [R, NB], [1, over]]),
                                      free_view(summed, at, [[NB * SPAN, 2], [SPAN, NB], [1, over]]),
                                      free_view(summed, at + R, [[NB * SPAN, 2], [SPAN, NB], [1, over]]), ALU.add)
                    dve.tensor_copy(free_view(mixT, m_at + over, [[m_step, 2], [R, NB], [1, R - over]]),
                                    free_view(summed, at + over, [[NB * SPAN, 2], [SPAN, NB], [1, R - over]])
                                    ).then_inc(mix_ready, 1)

                def reduce_piece(T, k, c, n_in_tile):
                    if not is_tile(T, 0) or c > 2:
                        dve.wait_ge(mix_ready, 3 * T + c - 2)
                    dve.wait_ge(y_used, 4 * T + n_in_tile + 3)
                    add_terms((k + c) % 2, n_in_tile % 2)

                def add_mix(T):
                    dve.wait_ge(out_turned, T + 1)
                    dve.scalar_tensor_tensor(out=xtile(T), in0=ps_o[:], scalar=gate_tanh[:, 0:1], in1=xtile(T),
                                             op0=ALU.mult, op1=ALU.add).then_inc(y1_ready, 1)

                def tile(i, k, ahead, group_done):
                    T = GT * i + k
                    before, final = not is_tile(T, 0), is_tile(T, NT - 1)
                    if before:
                        dve.wait_ge(terms_added, T)
                    products(T, k, 0, 1)
                    if before and not final:
                        add_mix(T - 1)
                    reduce_piece(T, k, 2, 1)
                    if before and not final:
                        row_stats(dve, T - 1, (k - 1) % GT)
                    products(T, k, 1, 0)
                    fold(T, k, 2, 0, 1)
                    if before and not final:
                        combine_stats(dve, T - 1, (k - 1) % GT)
                    if is_tile(T, 0):
                        first_stats(2)
                    products(T, k, 1, 1)
                    if final:
                        add_mix(T - 1)
                    reduce_piece(T, k, 3, 2)
                    fold(T, k, 3, 1, 0)
                    if is_tile(T, 0):
                        first_stats(3)
                    if ahead:
                        dve.wait_ge(qT_ready, T + 2)
                        products(T + 1, k + 1, 0, 0)
                        reduce_piece(T + 1, k + 1, 1, 0)
                    if group_done:
                        dve.wait_ge(rstd2, i)
                    if ahead:
                        fold(T + 1, k + 1, 1, 0, 0)

                dve.wait_ge(dma_taps_in, 32)
                dve.wait_ge(taps_zero, 1)
                dve.tensor_tensor(taps_sb[:, PAD:PAD + 1], taps_sb[:, PAD:PAD + 1], skip_sb[:], ALU.add
                                  ).then_inc(taps_ready, 1)
                dve.sem_inc(y_used, Y_CREDIT)
                first_stats(0)
                first_stats(1)
                dve.wait_ge(prod_zero, 1)
                dve.wait_ge(qT_ready, 1)
                products(0, 0, 0, 0)
                reduce_piece(0, 0, 1, 0)
                fold(0, 0, 1, 0, 0)
                dve.wait_ge(tanh_ready, 1)
                over_tiles(dve, tile)
                add_mix(NT - 1)

        with ExitStack() as scope:
            hold_weights(RESIDENT, NH, scope, "b")
            xT_hi = sb("xT_hi", [P, LC, 512], F32R, scope)
            xT_lo = sb("xT_lo", [P, LC, 512], F32R, scope)
            h_full = sb("h_full", [P, 2, 512], F32, scope)
            h_hi = sb("h_hi", [P, 2, 512], F32R, scope)
            h_lo = sb("h_lo", [P, 2, 512], F32R, scope)
            vec = sb("vec", [P, 3, D], F32, scope)
            st3 = sb("st3", [P, GT, 6], F32, scope)
            mv3 = sb("mv3", [P, GT, 2], F32, scope)
            ln3 = sb("ln3", [P, 4, GT], F32, scope)
            acc = scope.enter_context(nc.psum_tensor("acc", [P, GT, 512], F32))
            ps_h = scope.enter_context(nc.psum_tensor("ps_h", [P, 2, 512], F32))
            ps_t = scope.enter_context(nc.psum_tensor("ps_t", [P, 2, 512], F32))
            block = scope.enter_context(nc.Block())

            def stage_value(layer, s):
                if isinstance(layer, int) and layer == 0:
                    return 16 * ((s - EARLY) // WSLOTS + 1)
                return 16 * ((HALVES - EARLY) // WSLOTS + (HALVES // WSLOTS) * (layer - 1) + s // WSLOTS + 1)

            def weight_lo_on(eng, L, t):
                for half, hi, lo in ((0, w1_hi, w1_lo), (1, w2_hi, w2_lo)):
                    s = 2 * t + half
                    eng.wait_ge(w_hi_ready, HALVES * L + s + 1)
                    eng.tensor_tensor(lo[t], wstage[:, s % WSLOTS, :], hi[t].bitcast(F32), ALU.subtract
                                      ).then_inc(w_ready, 1)

            @block.sync
            def _(sp):
                def load_vectors(L, norm):
                    sp.dma_start(vec[:, 0, :], across(bias2, L)).then_inc(dma_vec, 16)
                    if norm:
                        sp.dma_start(vec[:, 1, :], across(gamma, L)).then_inc(dma_vec, 16)
                        sp.dma_start(vec[:, 2, :], across(beta, L)).then_inc(dma_vec, 16)

                def across(table, L):
                    row = table[bass.ds(L, 1)]
                    return bass.AP(tensor=row.tensor, offset=row.offset, ap=[[0, P], [1, D]])

                store_y1(sp, NT - 1, GT - 1)
                load_vectors(0, True)
                for s in range(EARLY + WSLOTS, HALVES):
                    load_half(sp, 0, s, True)

                def layer(L, last_norm):
                    for s in range(HALVES):
                        load_half(sp, L + 1, s, True)
                    sp.wait_ge(x_ready, NT * (L + 2))
                    load_vectors(L + 1, not last_norm)

                with sp.Fori(0, NL - 2) as L:
                    layer(L, False)
                layer(NL - 2, True)
                sp.wait_ge(w_ready, CREDIT + HALVES * NL)
                for g in range(NG):
                    if g:
                        sp.wait_ge(fin_ready, GT * g)
                    sp.dma_start(wstage[:, :, :], y1_dram[GT * g:GT * g + GT].rearrange("t p d -> p t d")
                                 ).then_inc(dma_base, 16)
                    for T in range(GT * g, GT * g + GT):
                        sp.wait_ge(fin_ready, T + 1)
                        sp.dma_start(out[T], xres[:, T, :]).then_inc(dma_out, 16)
                sp.wait_ge(dma_out, 16 * NT)

            @block.tensor
            def _(pe):
                def turn(n, g, c):
                    if c == 0:
                        pe.wait_ge(x_ready, GT * n + GT)
                    elif c >= 2:
                        pe.wait_ge(xT_ready, LC * n + c - 1)
                    for j in range(GT):
                        last = pe.transpose(ps_t[:, c % 2, j * P:(j + 1) * P], xres[:, GT * g + j, c * P:(c + 1) * P],
                                            ident[:])
                    last.then_inc(x_turned, 1)

                def up(L, n, g, t):
                    if g == 0:
                        pe.wait_ge(w_ready, CREDIT + HALVES * L + 2 * t + 1)
                    for c in range(LC):
                        if t == 0:
                            pe.wait_ge(xT_ready, LC * n + c + 1)
                        cs = slice(c * P, (c + 1) * P)
                        pe.matmul(ps_h[:, t % 2, :], w1_hi[t][:, cs], xT_hi[:, c, :], start=(c == 0), stop=False)
                        pe.matmul(ps_h[:, t % 2, :], w1_hi[t][:, cs], xT_lo[:, c, :], start=False, stop=False)
                        last = pe.matmul(ps_h[:, t % 2, :], w1_lo[t][:, cs], xT_hi[:, c, :], start=False,
                                         stop=(c == LC - 1))
                    last.then_inc(mm1_done, 1)

                def down(L, n, g, t, tiles):
                    if g == 0:
                        pe.wait_ge(w_ready, CREDIT + HALVES * L + 2 * t + 2)
                    pe.wait_ge(h_ready, NH * n + t + 1)
                    for j in tiles:
                        if t == 0:
                            pe.wait_ge(acc_free, GT * n + j + 1)
                        js = slice(j * P, (j + 1) * P)
                        pe.matmul(acc[:, j, :], h_hi[:, t % 2, js], w2_hi[t], start=(t == 0), stop=False)
                        pe.matmul(acc[:, j, :], h_hi[:, t % 2, js], w2_lo[t], start=False, stop=False)
                        last = pe.matmul(acc[:, j, :], h_lo[:, t % 2, js], w2_hi[t], start=False, stop=(t == NH - 1))
                        if t == NH - 1:
                            last.then_inc(mm2_done, 1)
                    if t < NH - 1:
                        last.then_inc(mm2_done, 1)

                def group(L, g, more):
                    n = NG * L + g
                    for t in range(NH):
                        up(L, n, g, t)
                        if t:
                            down(L, n, g, t - 1, range(GT))
                    if more:
                        g2 = (g + 1) % NG
                        turn(n + 1, g2, 0)
                        turn(n + 1, g2, 1)
                        down(L, n, g, NH - 1, [0, 1])
                        turn(n + 1, g2, 2)
                        down(L, n, g, NH - 1, [2])
                        turn(n + 1, g2, 3)
                        down(L, n, g, NH - 1, [3])
                    else:
                        down(L, n, g, NH - 1, range(GT))

                for c in range(LC):
                    turn(0, 0, c)
                with pe.Fori(0, NL - 1) as L:
                    for g in range(NG):
                        group(L, g, True)
                for g in range(NG):
                    group(NL - 1, g, g < NG - 1)

            @block.scalar
            def _(act):
                def weight_hi(L, t):
                    for half, table in ((0, w1_hi), (1, w2_hi)):
                        s = 2 * t + half
                        act.wait_ge(dma_w[s % WSLOTS], stage_value(L, s))
                        act.activation(table[t], wstage[:, s % WSLOTS, :], ACT.Copy).then_inc(w_hi_ready, 1)

                def input_hi(n, c):
                    act.wait_ge(x_turned, LC * n + c + 1)
                    act.activation(xT_hi[:, c, :], ps_t[:, c % 2, :], ACT.Copy).then_inc(xT_hi_ready, 1)

                def gelu(L, n, t):
                    act.wait_ge(mm1_done, NH * n + t + 1)
                    bias = b1[:, bass.ds(NH * L + t, 1)]
                    standalone(act)
                    act.activation(h_hi[:, t % 2, :], ps_h[:, t % 2, :], ACT.Gelu, bias=bias)
                    act.activation(h_full[:, t % 2, :], ps_h[:, t % 2, :], ACT.Gelu, bias=bias).then_inc(gelu_done, 1)

                def group(L, g, more, reload):
                    n = NG * L + g
                    for t in range(1, NH):
                        gelu(L, n, t)
                        if reload and t >= 2:
                            weight_hi(L + 1, t - 2)
                    if more:
                        input_hi(n + 1, 0)
                        input_hi(n + 1, 1)
                    if reload:
                        act.wait_ge(mm2_done, MM2 * n + NH - 1)
                        weight_hi(L + 1, NH - 2)
                    if more:
                        input_hi(n + 1, 2)
                        input_hi(n + 1, 3)
                    if reload:
                        act.wait_ge(mm2_done, MM2 * n + MM2)
                        weight_hi(L + 1, NH - 1)
                    if more:
                        gelu(L + (g + 1) // NG, n + 1, 0)

                act.activation(table_first[:], gate_tanh[:, 0:1], ACT.Gelu)
                for c in range(LC):
                    input_hi(0, c)
                for t in range(RESIDENT, NH):
                    if t == RESIDENT + 1:
                        gelu(0, 0, 0)
                    weight_hi(0, t)
                with act.Fori(0, NL - 1) as L:
                    for g in range(NG):
                        group(L, g, True, g == NG - 1)
                for g in range(NG):
                    group(NL - 1, g, g < NG - 1, False)

            @block.vector
            def _(dve):
                def weight_lo(L, t):
                    weight_lo_on(dve, L, t)

                def input_lo(n, c):
                    dve.wait_ge(xT_hi_ready, LC * n + c + 1)
                    dve.tensor_tensor(xT_lo[:, c, :], ps_t[:, c % 2, :], xT_hi[:, c, :].bitcast(F32), ALU.subtract
                                      ).then_inc(xT_ready, 1)

                def read_out(n, g, j):
                    dve.wait_ge(mm2_done, MM2 * n + NH - 1 + j + 1)
                    dve.wait_ge(biased, GT * n + j + 1)
                    dve.tensor_tensor(xres[:, GT * g + j, :], acc[:, j, :], xres[:, GT * g + j, :], ALU.add
                                      ).then_inc(acc_free, 1)

                def tile_stats(n, g, j):
                    dve.wait_ge(acc_free, GT * (n + 1) + j + 1)
                    dve.bn_stats(st3[:, j, :], xres[:, GT * g + j, :]).then_inc(st3_ready, 1)

                def finish(n, g, j):
                    dve.wait_ge(acc_free, GT * (n + 1) + j + 1)
                    if j == 0:
                        dve.wait_ge(dma_base, 16 * (g + 1))
                    dve.scalar_tensor_tensor(out=xres[:, GT * g + j, :], in0=xres[:, GT * g + j, :],
                                             scalar=gate_tanh[:, 1:2], in1=wstage[:, j, :], op0=ALU.mult,
                                             op1=ALU.add).then_inc(fin_ready, 1)

                def hidden_lo(n, t):
                    dve.wait_ge(gelu_done, NH * n + t + 1)
                    dve.tensor_tensor(h_lo[:, t % 2, :], h_full[:, t % 2, :], h_hi[:, t % 2, :].bitcast(F32),
                                      ALU.subtract).then_inc(h_ready, 1)

                def group(L, g, more, reload, norm):
                    n = NG * L + g
                    for t in range(1, NH):
                        hidden_lo(n, t)
                        if reload and t >= 2:
                            weight_lo(L + 1, t - 2)
                    close = tile_stats if norm else finish
                    steps = [(input_lo, 0), (input_lo, 1), (read_out, 0), (input_lo, 2), (read_out, 1), (close, 0),
                             (input_lo, 3), (read_out, 2), (close, 1), (read_out, 3), (hidden_lo, 0), (close, 2),
                             (close, 3)]
                    for step, a in steps:
                        if step is input_lo or step is hidden_lo:
                            if more:
                                step(n + 1, a)
                        else:
                            step(n, g, a)
                    if norm:
                        dve.wait_ge(st3_ready, GT * n + GT)
                        standalone(dve)
                        for j in range(GT):
                            last = dve.bn_aggr(mv3[:, j, :], st3[:, j, :])
                        last.then_inc(stats3, 1)
                dve.sem_inc(acc_free, GT)
                for c in range(LC):
                    input_lo(0, c)
                for k in range(GT - 2, GT):
                    row_stats(dve, NT - GT + k, k)
                for k in range(GT - 2, GT):
                    combine_stats(dve, NT - GT + k, k)
                for t in range(RESIDENT, NH):
                    if t == RESIDENT + 1:
                        hidden_lo(0, 0)
                    weight_lo(0, t)
                with dve.Fori(0, NL - 1) as L:
                    for g in range(NG):
                        group(L, g, True, g == NG - 1, True)
                for g in range(NG):
                    group(NL - 1, g, g < NG - 1, False, False)

            @block.gpsimd
            def _(pool):
                base = (len(X_STATS) + NG) * CH
                per = CH + 2

                def group(L, g, norm):
                    n = NG * L + g
                    pool.wait_ge(x_turned, LC * n + LC)
                    if norm:
                        pool.wait_ge(dma_vec, 48 * L + 48)
                    else:
                        pool.wait_ge(dma_vec, 48 * L + 16)
                    for j in range(GT):
                        xj = xres[:, GT * g + j, :]
                        pool.tensor_tensor(xj, xj, vec[:, 0, :], ALU.add).then_inc(biased, 1)
                    if not norm:
                        return
                    if g == NG - 1:
                        pool.wait_ge(w_ready, CREDIT + HALVES * (L + 1) + 2 * NH - 4)
                        weight_lo_on(pool, L + 1, NH - 2)
                        weight_lo_on(pool, L + 1, NH - 1)
                    link, k = linker(pool, pool_chain, base + per * n)
                    pool.wait_ge(stats3, n + 1)
                    rs, nm = ln3[:, 2, :], ln3[:, 3, :]
                    ln_done = rstd_chain(pool, link, mv3[:, :, 0], mv3[:, :, 1], ln3[:, 0, :], ln3[:, 1, :], rs, nm)
                    link(ln_done)
                    standalone(pool)
                    for j in range(GT):
                        xj = xres[:, GT * g + j, :]
                        last = pool.tensor_scalar(xj, xj, rs[:, j:j + 1], nm[:, j:j + 1], ALU.mult, ALU.add)
                    link(last)
                    for j in range(GT):
                        xj = xres[:, GT * g + j, :]
                        last = pool.tensor_tensor(xj, xj, vec[:, 1, :], ALU.mult)
                    last.then_inc(scaled, 1)
                    pool.wait_ge(scaled, n + 1)
                    for j in range(GT):
                        xj = xres[:, GT * g + j, :]
                        pool.tensor_tensor(xj, xj, vec[:, 2, :], ALU.add).then_inc(x_ready, 1)
                    assert k[0] == per

                second_rstd(pool, NG - 1)
                pool.wait_ge(rstd2, NG)
                for k in range(GT):
                    pool.wait_ge(dma_y1[k], 16 * NG)
                for k in range(GT):
                    xk = xres[:, NT - GT + k, :]
                    pool.tensor_scalar(xk, xk, ln2[:, 2, k:k + 1], ln2[:, 3, k:k + 1], ALU.mult, ALU.add
                                       ).then_inc(x_ready, 1)
                with pool.Fori(0, NL - 1) as L:
                    for g in range(NG):
                        group(L, g, True)
                for g in range(NG):
                    group(NL - 1, g, False)


def kernel(**inputs):
    import numpy as _np
    import concourse.bacc as _bacc
    from concourse import mybir as _mybir
    from concourse.bass_utils import run_bass_kernel_spmd as _run

    a = {k: _np.asarray(v) for k, v in inputs.items()}
    x, c = a["x"], a["ctx_2048"]
    B, S, D = x.shape
    R, NT = 8, B * S // 128

    def tiles(m):
        return m.reshape(B, NT, 2, R, D).transpose(1, 2, 0, 3, 4).reshape(NT, 128, D)

    w1, w2 = a["L0_ffn_W1"], a["L0_ffn_W2"]
    NL, H, _ = w1.shape
    LC, NH = D // 128, H // 128
    w1t = w1.reshape(NL, NH, 128, LC, 128).transpose(0, 1, 4, 3, 2).reshape(NL, NH, 1, 128, D)
    w2t = w2.reshape(NL, D, NH, 128).transpose(0, 2, 3, 1).reshape(NL, NH, 1, 128, D)
    arrays = {
        "x": tiles(x),
        "ctx_in": tiles(c.reshape(B, S, LC, 128)[..., ::-1].reshape(B, S, D)),
        "gates": _np.concatenate([a["g_xattn"], a["g_ffn"]]),
        "taps": a["L0_xattn_ssm_kernel"],
        "skip": a["L0_xattn_D"].reshape(-1, 1),
        "weights": _np.concatenate([w1t, w2t], axis=2),
        "bias1": a["L0_ffn_B1"].reshape(NL, NH, 128).transpose(2, 0, 1).reshape(128, NL * NH),
        "bias2": a["L0_ffn_B2"],
        "gamma": a["L0_ffn_LN_G"],
        "beta": a["L0_ffn_LN_B"],
    }
    arrays = {k: _np.ascontiguousarray(v) for k, v in arrays.items()}
    nc = _bacc.Bacc("TRN2", target_bir_lowering=False, num_devices=1)
    args = [nc.dram_tensor(k, v.shape, _mybir.dt.float32, kind="ExternalInput").ap() for k, v in arrays.items()]
    args.append(nc.dram_tensor("mixed_out", (NT, 128, D), _mybir.dt.float32, kind="ExternalOutput").ap())
    mixer_mlp_kernel(nc, *args)
    r = _run(nc, [arrays], core_ids=[0])
    y = r.results[0]["mixed_out"]
    return y.reshape(NT, 2, B, R, D).transpose(2, 0, 1, 3, 4).reshape(B, S, D)
```
